# Optimizing a Trainium2 kernel written in Bass

```python
import numpy as np
import jax
import jax.numpy as jnp

def _softmax(x, axis=-1):
    return jax.nn.softmax(x, axis=axis)

def _gelu(x):
    return jax.nn.gelu(x, approximate=True)

def _silu(x):
    return jax.nn.silu(x)

def _sigmoid(x):
    return jax.nn.sigmoid(x)

def _layernorm(x, axis=-1, eps=1e-05):
    m = jnp.mean(x, axis=axis, keepdims=True)
    v = jnp.var(x, axis=axis, keepdims=True)
    return (x - m) / jnp.sqrt(v + eps)

def _scatter_add(tgt, idx, src, axis=0):
    return tgt.at[idx].add(src)

def _segment_sum(src, seg, n):
    return jax.ops.segment_sum(src, seg, n)
kernel_name = 'mk_adj_preln_d2_adj_r2_5ff6a1'

def setup_inputs(seed: int=0):
    np.random.seed(seed)
    _w = jnp.asarray

    def _rec_inputs():
        import jax
        import jax.numpy as jnp
        _gk = jax.random.key(seed)
        x = -0.0002928 + 1 * jax.random.normal(jax.random.fold_in(_gk, 1), (16, 512, 128), jnp.float32)
        _a = jax.random.bernoulli(jax.random.fold_in(_gk, 2), 0.0078125, (512, 512))
        adj = _a.astype(jnp.int32)
        return (x, adj)
    x, adj = _rec_inputs()

    def _L0_gnn_setup():
        import jax, jax.numpy as jnp
        import numpy as np
        ALPHA = 0.2
        NEG_INF = -9000000000000000.0

        def _gat(inp, adj_mask, W, a):
            h = jnp.matmul(inp, W)
            F_ = h.shape[-1]
            f1 = jnp.matmul(h, a[:F_, 0])
            f2 = jnp.matmul(h, a[F_:, 0])
            e = jax.nn.leaky_relu(f1[:, :, None] + f2[:, None, :], ALPHA)
            if adj_mask is not None:
                e = jnp.where(adj_mask[None, :, :] > 0, e, NEG_INF)
            att = jax.nn.softmax(e, axis=2)
            h_prime = jnp.einsum('bij,bjf->bif', att, h)
            return jax.nn.elu(h_prime)
        key = jax.random.key(seed)
        ks = jax.random.split(key, 10)
        B, N, Fin, H, O = (16, 512, 128, 256, 128)

        def xavier(k, shape):
            fan_in, fan_out = (shape[0], shape[-1])
            bound = 1.414 * np.sqrt(6.0 / (fan_in + fan_out))
            return jax.random.uniform(k, shape, jnp.float32, -bound, bound)
        return {'x': jax.random.normal(ks[0], (B, N, Fin), jnp.float32), 'adj': jax.random.randint(ks[1], (N, N), 0, 2, jnp.int32), 'mlp1_w': xavier(ks[2], (Fin, H)), 'mlp1_b': jnp.zeros((H,), jnp.float32), 'mlp2_w': xavier(ks[3], (H, O)), 'mlp2_b': jnp.zeros((O,), jnp.float32), 'W_fc': xavier(ks[4], (H, H)), 'a_fc': xavier(ks[5], (2 * H, 1)), 'W_hand': xavier(ks[6], (O, O)), 'a_hand': xavier(ks[7], (2 * O, 1))}
    _L0_gnn_all = _L0_gnn_setup()
    _L0_gnn_in = {k: v for k, v in _L0_gnn_all.items() if k in ('mlp1_w', 'mlp1_b', 'mlp2_w', 'mlp2_b', 'W_fc', 'a_fc', 'W_hand', 'a_hand')}
    del _L0_gnn_all

    def _L1_gnn_setup():
        import jax, jax.numpy as jnp
        import numpy as np
        NEG_BIG = -9000000000000000.0
        key = jax.random.key(seed)
        k1, k2, k3, k4 = jax.random.split(key, 4)
        bs, N, Fin, Fout = (8, 1024, 128, 128)
        x = jax.random.normal(k1, (bs, N, Fin), dtype=jnp.float32)
        adj = jax.random.randint(k2, (N, N), 0, 2, dtype=jnp.int32)
        W = jax.random.normal(k3, (Fin, Fout), dtype=jnp.float32) * (1.414 / np.sqrt(Fin))
        a = jax.random.normal(k4, (2 * Fout, 1), dtype=jnp.float32) * 0.1
        return {'x': x, 'adj': adj, 'W': W, 'a': a}
    _L1_gnn_all = _L1_gnn_setup()
    _L1_gnn_in = {k: v for k, v in _L1_gnn_all.items() if k in ('W', 'a')}
    del _L1_gnn_all
    return {'x': x, 'adj': adj, 'L0_gnn_mlp1_w': _L0_gnn_in['mlp1_w'], 'L0_gnn_mlp1_b': _L0_gnn_in['mlp1_b'], 'L0_gnn_mlp2_w': _L0_gnn_in['mlp2_w'], 'L0_gnn_mlp2_b': _L0_gnn_in['mlp2_b'], 'L0_gnn_W_fc': _L0_gnn_in['W_fc'], 'L0_gnn_a_fc': _L0_gnn_in['a_fc'], 'L0_gnn_W_hand': _L0_gnn_in['W_hand'], 'L0_gnn_a_hand': _L0_gnn_in['a_hand'], 'L1_gnn_W': _L1_gnn_in['W'], 'L1_gnn_a': _L1_gnn_in['a']}

def reference(x, adj, L0_gnn_mlp1_w, L0_gnn_mlp1_b, L0_gnn_mlp2_w, L0_gnn_mlp2_b, L0_gnn_W_fc, L0_gnn_a_fc, L0_gnn_W_hand, L0_gnn_a_hand, L1_gnn_W, L1_gnn_a):
    import jax
    import jax.numpy as jnp

    def _L0_gnn_ref(x, adj, mlp1_w, mlp1_b, mlp2_w, mlp2_b, W_fc, a_fc, W_hand, a_hand):
        import jax, jax.numpy as jnp
        import numpy as np
        ALPHA = 0.2
        NEG_INF = -9000000000000000.0

        def _gat(inp, adj_mask, W, a):
            h = jnp.matmul(inp, W)
            F_ = h.shape[-1]
            f1 = jnp.matmul(h, a[:F_, 0])
            f2 = jnp.matmul(h, a[F_:, 0])
            e = jax.nn.leaky_relu(f1[:, :, None] + f2[:, None, :], ALPHA)
            if adj_mask is not None:
                e = jnp.where(adj_mask[None, :, :] > 0, e, NEG_INF)
            att = jax.nn.softmax(e, axis=2)
            h_prime = jnp.einsum('bij,bjf->bif', att, h)
            return jax.nn.elu(h_prime)
        out = jax.nn.relu(jnp.matmul(x, mlp1_w) + mlp1_b)
        residual = out
        out = _gat(jax.nn.relu(out), None, W_fc, a_fc)
        out = jax.nn.elu(out) + residual
        out = jax.nn.relu(jnp.matmul(out, mlp2_w) + mlp2_b)
        residual = out
        out = _gat(jax.nn.relu(out), adj, W_hand, a_hand)
        out = jax.nn.elu(out) + residual
        return jax.nn.relu(out)

    def _L1_gnn_ref(x, adj, W, a):
        import jax, jax.numpy as jnp
        import numpy as np
        NEG_BIG = -9000000000000000.0
        alpha = 0.2
        h = jnp.matmul(x, W)
        Fout = h.shape[-1]
        a1, a2 = (a[:Fout, 0], a[Fout:, 0])
        s1 = jnp.einsum('bnf,f->bn', h, a1)
        s2 = jnp.einsum('bnf,f->bn', h, a2)
        e = jax.nn.leaky_relu(s1[:, :, None] + s2[:, None, :], negative_slope=alpha)
        attention = jnp.where(adj[None, :, :] > 0, e, NEG_BIG)
        attention = jax.nn.softmax(attention, axis=-1)
        h_prime = jnp.matmul(attention, h)
        return jax.nn.elu(h_prime)
    h = jnp.maximum(_layernorm(x, axis=-1), 0.0)
    x = x + _L0_gnn_ref(h, adj, L0_gnn_mlp1_w, L0_gnn_mlp1_b, L0_gnn_mlp2_w, L0_gnn_mlp2_b, L0_gnn_W_fc, L0_gnn_a_fc, L0_gnn_W_hand, L0_gnn_a_hand)
    h = jnp.maximum(_layernorm(x, axis=-1), 0.0)
    x = x + _L1_gnn_ref(h, adj, L1_gnn_W, L1_gnn_a)
    return x

_drawn_inputs = setup_inputs


def setup_inputs(seed=0):
    import zlib

    import numpy as np

    out = dict(_drawn_inputs(seed))
    spreads = {'L0_gnn_mlp1_b': (0.0, 0.1), 'L0_gnn_mlp2_b': (0.0, 0.1)}
    factors = {'L0_gnn_a_hand': 3.28}
    for name, (base, spread) in spreads.items():
        noise = np.random.default_rng([zlib.crc32(name.encode()), seed]).standard_normal(out[name].shape)
        drawn = base * np.exp(spread * noise) if base else spread * noise
        out[name] = jnp.asarray(drawn.astype(out[name].dtype))
    for name, factor in factors.items():
        out[name] = (out[name] * factor).astype(out[name].dtype)
    return out
```

```python
import concourse.bass as bass
from concourse import mybir
from contextlib import ExitStack
import numpy as np

P = 128
SLOPE = 0.2
LN_EPS = 1e-5
MASKED = -9e15 / SLOPE
RANGE_LIMIT = 60.0
EMPTY_ARG = 69.0


class Batch:

    def __init__(self, half, slot, first):
        self.half, self.slot, self.first = half, slot, first
        self.n = half * 2 + slot


class Signal:

    def __init__(self, sem, per_batch):
        self.sem, self.per_batch = sem, per_batch

    def at(self, b, k):
        return self.sem, b.n * self.per_batch + k

    def before(self, b):
        return self.sem, b.n * self.per_batch

    def two_back(self, b):
        return self.sem, (b.n - 1) * self.per_batch


class SlotSignal:

    def __init__(self, sems):
        self.sems = sems

    def sem(self, b):
        return self.sems[b.slot]

    def landed(self, b):
        return self.sems[b.slot], (b.half + 1) * 16

    def two_back(self, b):
        return self.sems[b.slot], b.half * 16


def gnn_program(nc, x, adj, w1, b1, w2, b2, wfc, afc, whand, ahand, wl1, al1, out):
    fp32 = mybir.dt.float32
    i32 = mybir.dt.int32
    ALU = mybir.AluOpType
    ACT = mybir.ActivationFunctionType
    AX = mybir.AxisListType

    B, N, D = x.shape
    H = w1.shape[1]
    C = N // P
    HT = H // P
    assert C == 4 and HT == 2 and D == P and w2.shape[1] == P and B % 4 == 0

    ctx = ExitStack()
    with ctx:
        def sb(name, shape, dt=fp32):
            return ctx.enter_context(nc.sbuf_tensor(name, shape, dt))

        def semaphore(name):
            return ctx.enter_context(nc.semaphore(name))

        ident = sb("ident", [P, P])
        minus_half = sb("minus_half", [P, C])
        minus_one = sb("minus_one", [P, 1])
        w1_sb = sb("w1_sb", [P, H])
        b1_sb = sb("b1_sb", [P, HT])
        w2_sb = sb("w2_sb", [P, HT, D])
        b2_sb = sb("b2_sb", [P, 1])
        wfc_sb = sb("wfc_sb", [P, HT, H + 2])
        whand_sb = sb("whand_sb", [P, 1, D + 2])
        wl1_sb = sb("wl1_sb", [P, 1, D + 2])
        afc_sb = sb("afc_sb", [P, 2, H])
        ahand_sb = sb("ahand_sb", [P, 2, D])
        al1_sb = sb("al1_sb", [P, 2, D])
        wa_tmp = sb("wa_tmp", [P, 2, H])
        adj_sb = sb("adj_sb", [P, C, N], i32)
        edge = sb("edge", [P, C, N])
        edge_or_empty = sb("edge_or_empty", [P, C, N])
        has_edge = sb("has_edge", [P, C])
        empty = sb("empty", [P, C])
        empty_arg = sb("empty_arg", [P, C])
        mask_t = sb("mask_t", [P, C, N])
        guard = sb("guard", [P, 2, C])
        guard_col = sb("guard_col", [P, 1])
        guard_all = sb("guard_all", [P, 1])
        guard_flag = sb("guard_flag", [P, 1], i32)

        x_in = sb("x_in", [P, 2, C, D])
        x_res = sb("x_res", [P, 2, C, D])
        stats = sb("stats", [P, 2, 2, C, 6])
        meanvar = sb("meanvar", [P, 2, 2, C, 2])
        var_eps = sb("var_eps", [P, 2, 2, C])
        rstd = sb("rstd", [P, 2, 2, C])
        shift = sb("shift", [P, 2, 2, C])
        normed = [sb(f"normed{k}", [P, 2, C, D]) for k in range(2)]
        normed_t = [sb(f"normed_t{k}", [P, 2, N]) for k in range(2)]
        o1_t = sb("o1_t", [P, 2, HT, N])
        z_t = sb("z_t", [P, 2, HT, N])
        o2_t = sb("o2_t", [P, 2, N])
        x1 = sb("x1", [P, 2, C, D])
        y_out = sb("y_out", [P, 2, C, D])

        class Layer:

            def __init__(self, k, width, w):
                self.k, self.width, self.w = k, width, w
                self.masked = k > 0
                self.ext = sb(f"ext{k}", [P, 2, C, width + 4])
                self.fmax_col = sb(f"fmax_col{k}", [P, 2, 1])
                self.fmax = sb(f"fmax{k}", [P, 2, 1])
                self.pos = sb(f"pos{k}", [P, 2, C])
                self.args = sb(f"args{k}", [P, 2, 3 * C])
                self.uvb = sb(f"uvb{k}", [P, 2, 3 * C])
                self.row = sb(f"row{k}", [P, 2, N])
                self.prob = sb(f"prob{k}", [P, 2, C, N])
                self.recip = sb(f"recip{k}", [P, 2, C])
                self.y = sb(f"y{k}", [P, C, width])
                self.neg = sb(f"neg{k}", [P, C, width])
                self.u = sb(f"u{k}", [P, C, width])
                self.scratch = nc.dram_tensor(f"row_scratch{k}", [2, N], fp32, kind="Internal").ap()

        gat1 = Layer(0, H, wfc_sb)
        gat2 = Layer(1, D, whand_sb)
        gat3 = Layer(2, D, wl1_sb)
        layers = [gat1, gat2, gat3]

        bound = edge_or_empty
        score = edge[:, 0:2]
        prob_n = edge[:, 2:4]
        lrelu = adj_sb[:, 0:2].bitcast(fp32)
        minus_max = sb("minus_max", [P, 2, 1])

        bank = [ctx.enter_context(nc.psum_tensor(f"bank{k}", [P, 512], fp32)) for k in range(8)]

        x_v = x.rearrange("b (p c) d -> b p c d", c=C)
        out_v = out.rearrange("b (p c) d -> b p c d", c=C)

        s_load = semaphore("weights_loaded")
        s_adj = semaphore("adj_loaded")
        s_pool = semaphore("pool_constants")
        s_wa = semaphore("wa_chain")
        s_mask = semaphore("mask_chain")
        s_mt = semaphore("mask_transposed")
        s_mc = semaphore("mask_copied")

        with nc.Block() as block:
            @block.sync
            def _(sp):
                sp.dma_start(adj_sb[:], adj.rearrange("(p c) j -> p c j", c=C)).then_inc(s_adj, 16)
                loads = [
                    (afc_sb[:], afc.rearrange("(t f) o -> o t f", t=2).broadcast_to([P, 2, H])),
                    (ahand_sb[:], ahand.rearrange("(t f) o -> o t f", t=2).broadcast_to([P, 2, D])),
                    (al1_sb[:], al1.rearrange("(t f) o -> o t f", t=2).broadcast_to([P, 2, D])),
                    (wfc_sb[:, :, 2:H + 2], wfc.rearrange("(k p) f -> p k f", p=P)),
                    (whand_sb[:, 0, 2:D + 2], whand),
                    (wl1_sb[:, 0, 2:D + 2], wl1),
                    (w1_sb[:], w1),
                    (w2_sb[:], w2.rearrange("(k p) f -> p k f", p=P)),
                    *((b1_sb[:, k:k + 1], b1[k * P:(k + 1) * P].rearrange("(p o) -> p o", o=1)) for k in range(HT)),
                    (b2_sb[:], b2.rearrange("(p o) -> p o", o=1)),
                ]
                for dst, src in loads:
                    sp.dma_start(dst, src).then_inc(s_load, 16)
                sp.wait_ge(s_load, 16 * len(loads))

            @block.gpsimd
            def _(pool):
                nc.gpsimd.memset(ident[:], 0.0).then_inc(s_pool, 1)
                pool.wait_ge(s_pool, 1)
                nc.gpsimd.affine_select(out=ident[:], in_=ident[:], compare_op=ALU.not_equal, fill=1.0, base=0,
                                        pattern=[[-1, P]], channel_multiplier=1).then_inc(s_pool, 1)
                nc.gpsimd.memset(minus_half[:], -0.5).then_inc(s_pool, 1)
                nc.gpsimd.memset(minus_one[:], -1.0).then_inc(s_pool, 1)
                nc.gpsimd.memset(guard[:], 0.0).then_inc(s_pool, 1)
                for L in layers:
                    nc.gpsimd.memset(L.ext[:, :, :, L.width + 2:L.width + 3], 1.0).then_inc(s_pool, 1)
                pool.wait_ge(s_pool, 8)

            @block.vector
            def _(dve):
                dve.wait_ge(s_load, 16 * (9 + HT))
                done = 0
                for a_sb, w_sb, kt, width in ((afc_sb, wfc_sb, HT, H), (ahand_sb, whand_sb, 1, D), (al1_sb, wl1_sb, 1, D)):
                    for k in range(kt):
                        for t in range(2):
                            if done:
                                dve.wait_ge(s_wa, done)
                            nc.vector.tensor_tensor(wa_tmp[:, t, 0:width], w_sb[:, k, 2:width + 2], a_sb[:, t, :],
                                                    ALU.mult).then_inc(s_wa, 1)
                            dve.wait_ge(s_wa, done + 1)
                            nc.vector.tensor_reduce(w_sb[:, k, t:t + 1], wa_tmp[:, t, 0:width], AX.X,
                                                    ALU.add).then_inc(s_wa, 1)
                            done += 2
                dve.wait_ge(s_adj, 16)
                nc.vector.tensor_scalar(edge[:], adj_sb[:], 0.0, None, ALU.is_gt).then_inc(s_mask, 1)
                dve.wait_ge(s_mask, 1)
                nc.vector.tensor_reduce(has_edge[:], edge[:], AX.X, ALU.max).then_inc(s_mask, 1)
                dve.wait_ge(s_mask, 2)
                nc.vector.tensor_scalar(empty[:], has_edge[:], -1.0, 1.0, ALU.mult, ALU.add).then_inc(s_mask, 1)
                dve.wait_ge(s_mask, 3)
                nc.vector.tensor_scalar(empty_arg[:], empty[:], EMPTY_ARG + 1e4, -1e4, ALU.mult,
                                        ALU.add).then_inc(s_mask, 1)
                for c in range(C):
                    nc.vector.tensor_scalar(edge_or_empty[:, c, :], edge[:, c, :], empty[:, c:c + 1], None,
                                            ALU.max).then_inc(s_mask, 1)
                for t in range(C):
                    dve.wait_ge(s_mt, t + 1)
                    nc.vector.tensor_copy(mask_t[:, t, :], bank[t][:]).then_inc(s_mc, 1)
                nc.vector.tensor_scalar(bound[:], edge[:], 1e38, MASKED, ALU.mult, ALU.add).then_inc(s_mask, 1)
                dve.wait_ge(s_mask, 4 + C + 1)

            @block.tensor
            def _(pe):
                pe.wait_ge(s_pool, 2)
                pe.wait_ge(s_mask, 4 + C)
                for t in range(C):
                    for c in range(C):
                        last = nc.tensor.transpose(bank[t][:, c * P:(c + 1) * P],
                                                   edge_or_empty[:, c, t:N:C], ident[:])
                    last.then_inc(s_mt, 1)

        def network(tag, general, pipelined):

            def signal(name, per_batch):
                return Signal(semaphore(f"{tag}_{name}"), per_batch)

            def slots(name):
                return SlotSignal([semaphore(f"{tag}_{name}{k}") for k in range(2)])

            waited = {name: semaphore(f"{tag}_waited_{name}") for name in ("dve", "pool", "sp")}
            x_loaded = slots("x_loaded")
            xres_loaded = slots("xres_loaded")
            stored = slots("stored")
            stats_done = [signal(f"stats_done{k}", 4) for k in range(2)]
            aggr_done = [signal(f"aggr_done{k}", 4) for k in range(2)]
            var_ready = [signal(f"var_ready{k}", 1) for k in range(2)]
            rstd_ready = [signal(f"rstd_ready{k}", 1) for k in range(2)]
            shift_ready = [signal(f"shift_ready{k}", 1) for k in range(2)]
            normed_ready = [signal(f"normed_ready{k}", 4) for k in range(2)]
            norm_filled = [signal(f"norm_filled{k}", 1) for k in range(2)]
            norm_t_ready = [signal(f"norm_t_ready{k}", 1) for k in range(2)]
            o1_filled = signal("o1_filled", HT)
            o1_ready = signal("o1_ready", HT)
            z_filled = signal("z_filled", HT)
            z_ready = signal("z_ready", HT)
            o2_filled = signal("o2_filled", 1)
            o2_ready = signal("o2_ready", 1)
            o2n_filled = signal("o2n_filled", 1)
            v_ready = signal("v_ready", 1)
            x1_ready = signal("x1_ready", 1)
            y_ready = signal("y_ready", 1)

            class LayerSignals:
                def __init__(self, L):
                    k = L.k
                    parts = C if L is gat1 else C // 2
                    self.h_filled = signal(f"h_filled{k}", parts)
                    self.h_ready = signal(f"h_ready{k}", parts)
                    self.fmax_col = signal(f"fmax_col{k}", 1)
                    self.fmax = signal(f"fmax{k}", 1)
                    self.pos = signal(f"pos{k}", 1)
                    self.args = signal(f"args{k}", 3)
                    self.guarded = signal(f"guarded{k}", 1)
                    self.uvb = signal(f"uvb{k}", 1)
                    self.row_written = slots(f"row_written{k}")
                    self.row_loaded = slots(f"row_loaded{k}")
                    self.unmasked = signal(f"unmasked{k}", C)
                    self.prob_ready = signal(f"prob_ready{k}", C)
                    self.g_filled = signal(f"g_filled{k}", parts)
                    self.recip = signal(f"recip{k}", parts)
                    self.g_ready = signal(f"g_ready{k}", parts)
                    self.neg = signal(f"neg{k}", 2 if L is gat1 else 1)
                    self.exp = signal(f"exp{k}", 2 if L is gat1 else 1)
                    self.exp2 = signal(f"exp2{k}", 2 if L is gat1 else 1)
                    self.u = signal(f"u{k}", 2 if L is gat1 else 1)
                    if general and L.masked:
                        self.bounded = signal(f"bounded{k}", C)
                        self.shifted = signal(f"shifted{k}", C)
                        self.lrelu = signal(f"lrelu{k}", C)
                        self.minus_max = signal(f"minus_max{k}", C)
                        self.prob_n = signal(f"prob_n{k}", C)
                        self.prob_filled = signal(f"prob_filled{k}", C)

            sig = {L: LayerSignals(L) for L in layers}
            s1, s2, s3 = (sig[L] for L in layers)

            def factored(L):
                return not (general and L.masked)

            lagged = [
                ("prob1", 1), ("h2", 2), ("scores2", 2), ("attend1a", 1), ("norm1", 0), ("h3", 3), ("scores3", 3),
                ("attend1b", 1), ("prob2", 2), ("mlp1", 0), ("h1", 0), ("scores1", 0), ("mlp2", 1),
                ("prob3", 3), ("attend2", 2), ("norm2", 2), ("attend3", 3),
            ]
            lock_step = ["norm1", "mlp1", "h1", "scores1", "prob1", "attend1a", "attend1b", "mlp2",
                         "h2", "scores2", "prob2", "attend2", "norm2", "h3", "scores3", "prob3", "attend3"]

            def run(eng, steps):

                def turn(half, slot, first, live):
                    for name, lag in order:
                        if live(lag) and name in steps:
                            r = slot - lag
                            steps[name](Batch(half + r // 2, r % 2, first - lag))

                if not pipelined:
                    order = [(name, 0) for name in lock_step]
                    for t in range(2):
                        turn(0, t, t, lambda lag: True)
                    with eng.Fori(1, B // 2) as i:
                        for t in range(2):
                            turn(i, t, 2 + t, lambda lag: True)
                    return
                order = lagged
                deepest = max(lag for _, lag in order)
                for t in range(4):
                    turn(t // 2, t % 2, t, lambda lag: t >= lag)
                with eng.Fori(2, B // 2) as i:
                    for t in range(2):
                        turn(i, t, 4 + t, lambda lag: True)
                for t in range(B, B + deepest):
                    turn(t // 2, t % 2, t, lambda lag: t - lag < B)

            with nc.Block() as block:
                @block.sync
                def _(sp):
                    def load_x(b):
                        if b.first > 0:
                            sp.wait_ge(*normed_ready[0].two_back(b))
                        sp.dma_start(x_in[:, b.slot], x_v[b.n]).then_inc(x_loaded.sem(b), 16)

                    def load_x_again(b):
                        if b.first > 0:
                            sp.wait_ge(*x1_ready.two_back(b))
                        sp.dma_start(x_res[:, b.slot], x_v[b.n]).then_inc(xres_loaded.sem(b), 16)

                    def spread(b, L):
                        s = sig[L]
                        sp.wait_ge(*s.uvb.at(b, 1))
                        sp.sem_inc(waited["sp"], 1)
                        row = L.scratch[b.slot]
                        if b.first > 0:
                            sp.wait_ge(*s.row_loaded.two_back(b))
                        sp.dma_start(row.rearrange("(p c) -> p c", c=C),
                                     L.uvb[:, b.slot, 2 * C:3 * C]).then_inc(s.row_written.sem(b), 16)
                        sp.wait_ge(*s.row_written.landed(b))
                        sp.sem_inc(waited["sp"], 1)
                        if b.first > 0:
                            sp.wait_ge(*s.prob_ready.two_back(b))
                        sp.dma_start(L.row[:, b.slot],
                                     row.rearrange("(o n) -> o n", o=1).broadcast_to([P, N])).then_inc(
                            s.row_loaded.sem(b), 16)

                    def store(b):
                        sp.wait_ge(*y_ready.at(b, 1))
                        sp.dma_start(out_v[b.n], y_out[:, b.slot]).then_inc(stored.sem(b), 16)

                    run(sp, {
                        "norm1": load_x,
                        "scores1": lambda b: spread(b, gat1),
                        "h2": load_x_again,
                        "scores2": lambda b: spread(b, gat2),
                        "scores3": lambda b: spread(b, gat3),
                        "attend3": store,
                    })
                    for k in range(2):
                        sp.wait_ge(stored.sems[k], 16 * (B // 2))

                @block.gpsimd
                def _(pool):
                    def root(b, k):
                        pool.wait_ge(*var_ready[k].at(b, 1))
                        nc.gpsimd.tensor_tensor(rstd[:, b.slot, k], var_eps[:, b.slot, k], minus_half[:],
                                                ALU.pow).then_inc(rstd_ready[k].sem, 1)

                    def maximum(b, L):
                        s = sig[L]
                        if factored(L):
                            pool.wait_ge(*s.fmax_col.at(b, 1))
                            if b.first > 0:
                                pool.wait_ge(*s.args.two_back(b))
                            pool.sem_inc(waited["pool"], 1)
                            nc.gpsimd.partition_all_reduce(L.fmax[:, b.slot], L.fmax_col[:, b.slot], P,
                                                           bass.bass_isa.ReduceOp.max).then_inc(s.fmax.sem, 1)

                    run(pool, {
                        "norm1": lambda b: root(b, 0),
                        "norm2": lambda b: root(b, 1),
                        "scores1": lambda b: maximum(b, gat1),
                        "scores2": lambda b: maximum(b, gat2),
                        "scores3": lambda b: maximum(b, gat3),
                    })

                @block.scalar
                def _(act):
                    def relu_normed(b, k):
                        act.wait_ge(*norm_filled[k].at(b, 1))
                        if b.first > 0:
                            if k == 0:
                                act.wait_ge(*o1_filled.two_back(b))
                            else:
                                act.wait_ge(*s3.h_filled.two_back(b))
                        nc.scalar.activation(normed_t[k][:, b.slot], bank[6 * k][:], ACT.Relu).then_inc(
                            norm_t_ready[k].sem, 1)

                    def mlp1(b):
                        relu_normed(b, 0)
                        for f in range(HT):
                            act.wait_ge(*o1_filled.at(b, f + 1))
                            if b.first > 0 and f == 0:
                                act.wait_ge(*z_ready.two_back(b))
                                act.wait_ge(*s1.h_filled.two_back(b))
                            nc.scalar.activation(o1_t[:, b.slot, f], bank[1 - f][:], ACT.Relu,
                                                 bias=b1_sb[:, f:f + 1]).then_inc(o1_ready.sem, 1)

                    def h1(b):
                        for c in range(C):
                            act.wait_ge(*s1.h_filled.at(b, c + 1))
                            if b.first > 0 and c == 0:
                                act.wait_ge(*s1.g_filled.two_back(b))
                                act.wait_ge(*s1.args.two_back(b))
                            nc.scalar.activation(gat1.ext[:, b.slot, c, 0:H + 2], bank[(c + 1) % 2][:, 0:H + 2],
                                                 ACT.Copy).then_inc(s1.h_ready.sem, 1)

                    def h_masked(b, L, banks):
                        s = sig[L]
                        for q in range(C // 2):
                            act.wait_ge(*s.h_filled.at(b, q + 1))
                            if b.first > 0 and q == 0:
                                act.wait_ge(*s.g_filled.two_back(b))
                                if factored(L):
                                    act.wait_ge(*s.args.two_back(b))
                                else:
                                    act.wait_ge(*s.shifted.two_back(b))
                                    act.wait_ge(*s.uvb.two_back(b))
                            nc.scalar.activation(
                                L.ext[:, b.slot, 2 * q:2 * q + 2, 0:D + 2],
                                banks[q][:, 0:2 * (D + 2)].rearrange("p (t n) -> p t n", t=2),
                                ACT.Copy).then_inc(s.h_ready.sem, 1)

                    def h3(b):
                        relu_normed(b, 1)
                        h_masked(b, gat3, (bank[7], bank[6]))

                    def exponentials(b, L):
                        s = sig[L]
                        if factored(L):
                            act.wait_ge(*s.args.at(b, 3))
                            if b.first > 0:
                                act.wait_ge(*s.prob_ready.two_back(b))
                                act.wait_ge(*s.row_loaded.two_back(b))
                            nc.scalar.activation(L.uvb[:, b.slot], L.args[:, b.slot], ACT.Exp).then_inc(s.uvb.sem, 1)

                    def general_prob(b, L, banks):
                        s = sig[L]
                        for c in range(C):
                            act.wait_ge(*s.minus_max.at(b, c + 1))
                            if c >= 2:
                                act.wait_ge(*s.prob_filled.at(b, c - 1))
                            else:
                                act.wait_ge(*s.prob_filled.before(b))
                            nc.scalar.activation(prob_n[:, c % 2], lrelu[:, c % 2], ACT.Exp,
                                                 bias=minus_max[:, c % 2]).then_inc(s.prob_n.sem, 1)
                            act.wait_ge(*s.prob_filled.at(b, c + 1))
                            if b.first > 0:
                                act.wait_ge(*s.g_filled.two_back(b))
                            nc.scalar.activation(L.prob[:, b.slot, :, c * P:(c + 1) * P],
                                                 banks[c % 2][:].rearrange("p (t n) -> p t n", t=C),
                                                 ACT.Copy).then_inc(s.prob_ready.sem, 1)

                    def elu_twice(b, L, part, parts):
                        s = sig[L]
                        r = slice(part * C // parts, (part + 1) * C // parts)
                        act.wait_ge(*s.neg.at(b, part + 1))
                        nc.scalar.activation(L.neg[:, r], L.neg[:, r], ACT.Exp).then_inc(s.exp.sem, 1)
                        if L is gat3:
                            return
                        act.wait_ge(*s.exp.at(b, part + 1))
                        nc.scalar.activation(L.neg[:, r], L.neg[:, r], ACT.Exp, bias=minus_one[:]).then_inc(
                            s.exp2.sem, 1)

                    def mlp2(b):
                        act.wait_ge(*o2_filled.at(b, 1))
                        if b.first > 0:
                            act.wait_ge(*o2n_filled.two_back(b))
                        nc.scalar.activation(o2_t[:, b.slot], bank[2][:], ACT.Relu, bias=b2_sb[:]).then_inc(
                            o2_ready.sem, 1)

                    run(act, {
                        "mlp1": mlp1,
                        "h1": h1,
                        "scores1": lambda b: exponentials(b, gat1),
                        "attend1a": lambda b: elu_twice(b, gat1, 0, 2),
                        "attend1b": lambda b: elu_twice(b, gat1, 1, 2),
                        "mlp2": mlp2,
                        "h2": lambda b: h_masked(b, gat2, (bank[4], bank[5])),
                        "scores2": lambda b: exponentials(b, gat2),
                        "prob2": (lambda b: general_prob(b, gat2, (bank[4], bank[5]))) if general else (lambda b: None),
                        "attend2": lambda b: elu_twice(b, gat2, 0, 1),
                        "h3": h3,
                        "scores3": lambda b: exponentials(b, gat3),
                        "prob3": (lambda b: general_prob(b, gat3, (bank[7], bank[6]))) if general else (lambda b: None),
                        "attend3": lambda b: elu_twice(b, gat3, 0, 1),
                    })

                @block.vector
                def _(dve):
                    def norm(b, k, src):
                        st, mv = stats[:, b.slot, k], meanvar[:, b.slot, k]
                        for c in range(C):
                            nc.vector.bn_stats(st[:, c], src[:, c]).then_inc(stats_done[k].sem, 1)
                        dve.wait_ge(*stats_done[k].at(b, C))
                        dve.sem_inc(waited["dve"], 1)
                        for c in range(C):
                            nc.vector.bn_aggr(mv[:, c], st[:, c]).then_inc(aggr_done[k].sem, 1)
                        dve.wait_ge(*aggr_done[k].at(b, C))
                        nc.vector.tensor_scalar(var_eps[:, b.slot, k], mv[:, :, 1], LN_EPS, None, ALU.add).then_inc(
                            var_ready[k].sem, 1)
                        dve.wait_ge(*rstd_ready[k].at(b, 1))
                        nc.vector.scalar_tensor_tensor(out=shift[:, b.slot, k], in0=mv[:, :, 0], scalar=-1.0,
                                                       in1=rstd[:, b.slot, k], op0=ALU.mult, op1=ALU.mult).then_inc(
                            shift_ready[k].sem, 1)
                        dve.wait_ge(*shift_ready[k].at(b, 1))
                        if b.first > 0:
                            dve.wait_ge(*norm_filled[k].two_back(b))
                        for c in range(C):
                            nc.vector.tensor_scalar(normed[k][:, b.slot, c], src[:, c],
                                                    rstd[:, b.slot, k, c:c + 1], shift[:, b.slot, k, c:c + 1],
                                                    ALU.mult, ALU.add).then_inc(normed_ready[k].sem, 1)

                    def norm1(b):
                        dve.wait_ge(*x_loaded.landed(b))
                        norm(b, 0, x_in[:, b.slot])

                    def scores(b, L):
                        s = sig[L]
                        f1, f2 = L.ext[:, b.slot, :, 0], L.ext[:, b.slot, :, 1]
                        dve.wait_ge(*s.h_ready.at(b, s.h_ready.per_batch))
                        if not factored(L):
                            if b.first > 0:
                                dve.wait_ge(*s.row_loaded.two_back(b))
                            nc.vector.tensor_copy(L.uvb[:, b.slot, 2 * C:3 * C], f2).then_inc(s.uvb.sem, 1)
                            return
                        nc.vector.tensor_reduce(L.fmax_col[:, b.slot], f2, AX.X, ALU.max).then_inc(s.fmax_col.sem, 1)
                        dve.wait_ge(*s.fmax.at(b, 1))
                        top = L.fmax[:, b.slot]
                        a = L.args[:, b.slot]
                        if b.first > 0:
                            dve.wait_ge(*s.uvb.two_back(b))
                        nc.vector.tensor_scalar(L.pos[:, b.slot], f1, top, 0.0, ALU.add, ALU.max).then_inc(s.pos.sem, 1)
                        nc.vector.tensor_scalar(a[:, 0:C], f2, top, None, ALU.subtract).then_inc(s.args.sem, 1)
                        nc.vector.tensor_scalar(a[:, C:2 * C], f2, top, SLOPE, ALU.subtract, ALU.mult).then_inc(
                            s.args.sem, 1)
                        dve.wait_ge(*s.pos.at(b, 1))
                        if L.masked:
                            nc.vector.scalar_tensor_tensor(out=a[:, 2 * C:3 * C], in0=L.pos[:, b.slot],
                                                           scalar=SLOPE - 1.0, in1=empty_arg[:], op0=ALU.mult,
                                                           op1=ALU.max).then_inc(s.args.sem, 1)
                            g = guard[:, L.k - 1]
                            dve.wait_ge(*s.args.at(b, 1))
                            dve.wait_ge(*s.guarded.before(b))
                            nc.vector.tensor_tensor(g, g, a[:, 0:C], ALU.min).then_inc(s.guarded.sem, 1)
                        else:
                            nc.vector.tensor_scalar(a[:, 2 * C:3 * C], L.pos[:, b.slot], SLOPE - 1.0, None,
                                                    ALU.mult).then_inc(s.args.sem, 1)

                    def prob(b, L):
                        s = sig[L]
                        p = L.prob[:, b.slot]
                        dve.wait_ge(*s.row_loaded.landed(b))
                        dve.wait_ge(*s.uvb.at(b, 1))
                        if b.first > 0:
                            dve.wait_ge(*s.g_filled.two_back(b))
                        row = L.row[:, b.slot].rearrange("q (p c) -> q c p", c=C)
                        for t in range(C):
                            nc.vector.tensor_scalar(
                                p[:, t].rearrange("q (c p) -> q c p", c=C), row,
                                L.uvb[:, b.slot, C + t:C + t + 1], L.uvb[:, b.slot, t:t + 1],
                                ALU.mult, ALU.max).then_inc((s.unmasked if L.masked else s.prob_ready).sem, 1)
                        if L.masked:
                            for t in range(C):
                                dve.wait_ge(*s.unmasked.at(b, t + 1))
                                nc.vector.tensor_tensor(p[:, t], p[:, t], mask_t[:, t], ALU.min).then_inc(
                                    s.prob_ready.sem, 1)

                    def general_prob(b, L):
                        s = sig[L]
                        dve.wait_ge(*s.row_loaded.landed(b))
                        dve.wait_ge(*s.h_ready.at(b, s.h_ready.per_batch))
                        for c in range(C):
                            if c >= 2:
                                dve.wait_ge(*s.prob_n.at(b, c - 1))
                            else:
                                dve.wait_ge(*s.prob_n.before(b))
                            nc.vector.tensor_tensor(score[:, c % 2], L.row[:, b.slot], bound[:, c],
                                                    ALU.min).then_inc(s.bounded.sem, 1)
                            dve.wait_ge(*s.bounded.at(b, c + 1))
                            nc.vector.tensor_scalar(score[:, c % 2], score[:, c % 2], L.ext[:, b.slot, c, 0:1], None,
                                                    ALU.add).then_inc(s.shifted.sem, 1)
                            dve.wait_ge(*s.shifted.at(b, c + 1))
                            nc.vector.scalar_tensor_tensor(out=lrelu[:, c % 2], in0=score[:, c % 2], scalar=SLOPE,
                                                           in1=score[:, c % 2], op0=ALU.mult, op1=ALU.max).then_inc(
                                s.lrelu.sem, 1)
                            dve.wait_ge(*s.lrelu.at(b, c + 1))
                            nc.vector.tensor_reduce(minus_max[:, c % 2], lrelu[:, c % 2], AX.X, ALU.max,
                                                    negate=True).then_inc(s.minus_max.sem, 1)

                    def prob_step(b, L):
                        if factored(L):
                            prob(b, L)
                        else:
                            general_prob(b, L)

                    def attend1(b, part):
                        s, L = s1, gat1
                        for c in (2 * part, 2 * part + 1):
                            ps = bank[2 + c % 2]
                            dve.wait_ge(*s.g_filled.at(b, c + 1))
                            nc.vector.reciprocal(L.recip[:, b.slot, c:c + 1], ps[:, H:H + 1]).then_inc(s.recip.sem, 1)
                            dve.wait_ge(*s.recip.at(b, c + 1))
                            nc.vector.tensor_scalar(L.y[:, c], ps[:, 0:H], L.recip[:, b.slot, c:c + 1], None,
                                                    ALU.mult).then_inc(s.g_ready.sem, 1)
                        r = slice(2 * part, 2 * part + 2)
                        dve.wait_ge(*s.g_ready.at(b, 2 * part + 2))
                        nc.vector.tensor_scalar(L.neg[:, r], L.y[:, r], 0.0, None, ALU.min).then_inc(s.neg.sem, 1)

                    def finish1(b, part):
                        s, L = s1, gat1
                        r = slice(2 * part, 2 * part + 2)
                        dve.wait_ge(*s.exp2.at(b, part + 1))
                        dve.wait_ge(*z_filled.before(b))
                        nc.vector.scalar_tensor_tensor(out=L.u[:, r], in0=L.y[:, r], scalar=0.0, in1=L.neg[:, r],
                                                       op0=ALU.max, op1=ALU.add).then_inc(s.u.sem, 1)

                    def attend1b(b):
                        attend1(b, 1)
                        finish1(b, 0)

                    def mlp2(b):
                        finish1(b, 1)
                        for f in range(HT):
                            dve.wait_ge(*z_filled.at(b, f + 1))
                            if b.first > 0 and f == 0:
                                dve.wait_ge(*o2_filled.two_back(b))
                            nc.vector.scalar_tensor_tensor(out=z_t[:, b.slot, f], in0=bank[2 + f][:], scalar=-1.0,
                                                           in1=o1_t[:, b.slot, f], op0=ALU.add, op1=ALU.add).then_inc(
                                z_ready.sem, 1)

                    def attend_masked(b, L, banks):
                        s = sig[L]
                        for q in range(C // 2):
                            dve.wait_ge(*s.g_filled.at(b, q + 1))
                            ps = banks[q][:, 0:2 * (D + 2)].rearrange("p (t n) -> p t n", t=2)
                            rc = L.recip[:, b.slot, 2 * q:2 * q + 2]
                            nc.vector.reciprocal(rc, ps[:, :, D]).then_inc(s.recip.sem, 1)
                            dve.wait_ge(*s.recip.at(b, q + 1))
                            for e in range(2):
                                last = nc.vector.tensor_scalar(L.y[:, 2 * q + e], ps[:, e, 0:D],
                                                               L.recip[:, b.slot, 2 * q + e:2 * q + e + 1], None,
                                                               ALU.mult)
                            last.then_inc(s.g_ready.sem, 1)
                        dve.wait_ge(*s.g_ready.at(b, 2))
                        nc.vector.tensor_scalar(L.neg[:], L.y[:], 0.0, None, ALU.min).then_inc(s.neg.sem, 1)
                        dve.wait_ge(*(s.exp if L is gat3 else s.exp2).at(b, 1))
                        nc.vector.scalar_tensor_tensor(out=L.u[:], in0=L.y[:], scalar=0.0, in1=L.neg[:],
                                                       op0=ALU.max, op1=ALU.add).then_inc(s.u.sem, 1)
                        dve.wait_ge(*s.u.at(b, 1))

                    def attend2(b):
                        attend_masked(b, gat2, (bank[4], bank[5]))

                    def norm2(b):
                        dve.wait_ge(*o2n_filled.at(b, 1))
                        v = gat2.u[:].rearrange("p c n -> p (c n)")
                        nc.vector.scalar_tensor_tensor(out=v, in0=bank[4][:], scalar=-1.0, in1=v,
                                                       op0=ALU.add, op1=ALU.add).then_inc(v_ready.sem, 1)
                        dve.wait_ge(*v_ready.at(b, 1))
                        dve.wait_ge(*xres_loaded.landed(b))
                        if b.first > 0:
                            dve.wait_ge(*y_ready.two_back(b))
                        nc.vector.scalar_tensor_tensor(out=x1[:, b.slot], in0=gat2.u[:], scalar=0.0,
                                                       in1=x_res[:, b.slot], op0=ALU.max, op1=ALU.add).then_inc(
                            x1_ready.sem, 1)
                        dve.wait_ge(*x1_ready.at(b, 1))
                        norm(b, 1, x1[:, b.slot])

                    def attend3(b):
                        attend_masked(b, gat3, (bank[7], bank[6]))
                        if b.first > 0:
                            dve.wait_ge(*stored.two_back(b))
                        nc.vector.scalar_tensor_tensor(out=y_out[:, b.slot], in0=gat3.u[:], scalar=-1.0,
                                                       in1=x1[:, b.slot], op0=ALU.add, op1=ALU.add).then_inc(
                            y_ready.sem, 1)

                    run(dve, {
                        "norm1": norm1,
                        "scores1": lambda b: scores(b, gat1),
                        "prob1": lambda b: prob(b, gat1),
                        "attend1a": lambda b: attend1(b, 0),
                        "attend1b": attend1b,
                        "mlp2": mlp2,
                        "scores2": lambda b: scores(b, gat2),
                        "prob2": lambda b: prob_step(b, gat2),
                        "attend2": attend2,
                        "norm2": norm2,
                        "scores3": lambda b: scores(b, gat3),
                        "prob3": lambda b: prob_step(b, gat3),
                        "attend3": attend3,
                    })

                @block.tensor
                def _(pe):
                    def mlp1(b):
                        pe.wait_ge(*normed_ready[0].at(b, C))
                        pe.wait_ge(*s1.h_ready.before(b))
                        for c in range(C):
                            last = nc.tensor.transpose(bank[0][:, c * P:(c + 1) * P], normed[0][:, b.slot, c],
                                                       ident[:])
                        last.then_inc(norm_filled[0].sem, 1)
                        pe.wait_ge(*norm_t_ready[0].at(b, 1))
                        for f in range(HT):
                            nc.tensor.matmul(bank[1 - f][:], w1_sb[:, f * P:(f + 1) * P], normed_t[0][:, b.slot],
                                             start=True, stop=True).then_inc(o1_filled.sem, 1)

                    def h1(b):
                        pe.wait_ge(*o1_ready.at(b, HT))
                        for c in range(C):
                            if c >= 2:
                                pe.wait_ge(*s1.h_ready.at(b, c - 1))
                            for k in range(HT):
                                last = nc.tensor.matmul(bank[(c + 1) % 2][:, 0:H + 2],
                                                        o1_t[:, b.slot, k, c * P:(c + 1) * P], wfc_sb[:, k],
                                                        start=(k == 0), stop=(k == HT - 1))
                            last.then_inc(s1.h_filled.sem, 1)

                    def attend1(b, part):
                        for c in (2 * part, 2 * part + 1):
                            if c == 0:
                                pe.wait_ge(*o2_ready.before(b))
                                pe.wait_ge(*s1.h_ready.at(b, C))
                            elif c == 1:
                                pe.wait_ge(*z_ready.before(b))
                            else:
                                pe.wait_ge(*s1.g_ready.at(b, c - 1))
                            for t in range(C):
                                if c == 0:
                                    pe.wait_ge(*s1.prob_ready.at(b, t + 1))
                                last = nc.tensor.matmul(bank[2 + c % 2][:, 0:H + 1],
                                                        gat1.prob[:, b.slot, t, c * P:(c + 1) * P],
                                                        gat1.ext[:, b.slot, t, 2:H + 3],
                                                        start=(t == 0), stop=(t == C - 1))
                            last.then_inc(s1.g_filled.sem, 1)

                    def mlp2(b):
                        pe.wait_ge(*s1.u.at(b, 2))
                        for f in range(HT):
                            pe.wait_ge(*s1.g_ready.at(b, 3 + f))
                            for c in range(C):
                                last = nc.tensor.transpose(bank[2 + f][:, c * P:(c + 1) * P],
                                                           gat1.u[:, c, f * P:(f + 1) * P], ident[:])
                            last.then_inc(z_filled.sem, 1)
                        pe.wait_ge(*z_ready.at(b, HT))
                        for k in range(HT):
                            last = nc.tensor.matmul(bank[2][:], w2_sb[:, k], z_t[:, b.slot, k],
                                                    start=(k == 0), stop=(k == HT - 1))
                        last.then_inc(o2_filled.sem, 1)

                    def h_masked(b, L, src, banks):
                        s = sig[L]
                        for q in range(C // 2):
                            for e in range(2):
                                c = 2 * q + e
                                last = nc.tensor.matmul(banks[q][:, e * (D + 2):(e + 1) * (D + 2)],
                                                        src[:, c * P:(c + 1) * P], L.w[:, 0], start=True, stop=True)
                            last.then_inc(s.h_filled.sem, 1)

                    def h2(b):
                        pe.wait_ge(*o2_ready.at(b, 1))
                        pe.wait_ge(*v_ready.before(b))
                        pe.wait_ge(*s2.g_ready.before(b))
                        h_masked(b, gat2, o2_t[:, b.slot], (bank[4], bank[5]))

                    def h3(b):
                        pe.wait_ge(*normed_ready[1].at(b, C))
                        pe.wait_ge(*s3.g_ready.before(b))
                        for c in range(C):
                            last = nc.tensor.transpose(bank[6][:, c * P:(c + 1) * P], normed[1][:, b.slot, c],
                                                       ident[:])
                        last.then_inc(norm_filled[1].sem, 1)
                        pe.wait_ge(*norm_t_ready[1].at(b, 1))
                        h_masked(b, gat3, normed_t[1][:, b.slot], (bank[7], bank[6]))

                    def general_prob(b, L, banks):
                        s = sig[L]
                        for c in range(C):
                            pe.wait_ge(*s.prob_n.at(b, c + 1))
                            if c < 2:
                                pe.wait_ge(*s.h_ready.at(b, c + 1))
                            else:
                                pe.wait_ge(*s.prob_ready.at(b, c - 1))
                            for t in range(C):
                                last = nc.tensor.transpose(banks[c % 2][:, t * P:(t + 1) * P],
                                                           prob_n[:, c % 2, t:N:C], ident[:])
                            last.then_inc(s.prob_filled.sem, 1)

                    def attend_masked(b, L, banks):
                        s = sig[L]
                        pe.wait_ge(*s.h_ready.at(b, 2))
                        if not factored(L):
                            pe.wait_ge(*s.prob_ready.at(b, C))
                        for q in range(C // 2):
                            for e in range(2):
                                c = 2 * q + e
                                for t in range(C):
                                    if c == 0 and factored(L):
                                        pe.wait_ge(*s.prob_ready.at(b, t + 1))
                                    last = nc.tensor.matmul(banks[q][:, e * (D + 2):e * (D + 2) + D + 1],
                                                            L.prob[:, b.slot, t, c * P:(c + 1) * P],
                                                            L.ext[:, b.slot, t, 2:D + 3],
                                                            start=(t == 0), stop=(t == C - 1))
                            last.then_inc(s.g_filled.sem, 1)

                    def attend2(b):
                        attend_masked(b, gat2, (bank[4], bank[5]))
                        pe.wait_ge(*s2.g_ready.at(b, 1))
                        for c in range(C):
                            last = nc.tensor.transpose(bank[4][:, c * P:(c + 1) * P],
                                                       o2_t[:, b.slot, c * P:(c + 1) * P], ident[:])
                        last.then_inc(o2n_filled.sem, 1)

                    run(pe, {
                        "mlp1": mlp1,
                        "h1": h1,
                        "attend1a": lambda b: attend1(b, 0),
                        "attend1b": lambda b: attend1(b, 1),
                        "mlp2": mlp2,
                        "h2": h2,
                        "prob2": (lambda b: general_prob(b, gat2, (bank[4], bank[5]))) if general else (lambda b: None),
                        "attend2": attend2,
                        "h3": h3,
                        "prob3": (lambda b: general_prob(b, gat3, (bank[7], bank[6]))) if general else (lambda b: None),
                        "attend3": lambda b: attend_masked(b, gat3, (bank[7], bank[6])),
                    })

        MODE(network)


def MODE(network):
    network("g", general=True, pipelined=False)


_INS = ['x', 'adj', 'L0_gnn_mlp1_w', 'L0_gnn_mlp1_b', 'L0_gnn_mlp2_w', 'L0_gnn_mlp2_b', 'L0_gnn_W_fc', 'L0_gnn_a_fc',
        'L0_gnn_W_hand', 'L0_gnn_a_hand', 'L1_gnn_W', 'L1_gnn_a']
_OUTS = [((16, 512, 128), 'float32')]


def kernel(**inputs):
    import numpy as _np
    import concourse.bacc as _bacc
    from concourse import mybir as _mybir
    from concourse.bass_utils import run_bass_kernel_spmd as _run

    nc = _bacc.Bacc("TRN2", target_bir_lowering=False, num_devices=1)
    arrays, args = {}, []
    for name in _INS:
        a = _np.ascontiguousarray(inputs[name])
        arrays[f"in_{name}"] = a
        args.append(nc.dram_tensor(f"in_{name}", a.shape, _mybir.dt.from_np(a.dtype), kind="ExternalInput").ap())
    for i, (shape, dtype) in enumerate(_OUTS):
        dt = _mybir.dt.from_np(_np.dtype(dtype))
        args.append(nc.dram_tensor(f"out_{i}", shape, dt, kind="ExternalOutput").ap())
    gnn_program(nc, *args)
    r = _run(nc, [arrays], core_ids=[0])
    return r.results[0]["out_0"]
```

```python
import concourse.bass as bass
from concourse import mybir
from contextlib import ExitStack
import numpy as np

P = 128
SLOPE = 0.2
LN_EPS = 1e-5
MASKED = -9e15 / SLOPE
RANGE_LIMIT = 60.0
EMPTY_ARG = 69.0


LAGGED = [
    ("load", 0), ("max2", 3), ("args2", 3), ("mlp1", 1), ("norm1a", 0), ("h3", 4), ("max3", 4), ("h1", 1),
    ("args3", 4), ("norm1b", 0), ("prob2", 3), ("attend1a", 2), ("prob3", 4), ("attend1b", 2), ("elu1", 2),
    ("max1", 1), ("attend2", 3), ("args1", 1), ("z", 2), ("attend3a", 4), ("elu2", 3), ("mlp2", 2),
    ("norm2a", 3), ("attend3b", 4), ("mlp1_turn", 0), ("norm2b", 3), ("h2", 2), ("prob1", 1), ("turn2", 3),
    ("elu3", 4),
]


class Batch:

    def __init__(self, half, slot, first, passed):
        self.half, self.slot, self.first, self.passed = half, slot, first + passed, passed
        self.n = half * 2 + slot
        self.count = half * 2 + (slot + passed)


class Signal:

    def __init__(self, sem, per_batch, skipped=0):
        self.sem, self.per_batch, self.skipped = sem, per_batch, skipped

    def at(self, b, k):
        return self.sem, (b.count - self.skipped) * self.per_batch + k

    def before(self, b):
        return self.at(b, 0)

    def two_back(self, b):
        return self.at(b, -self.per_batch)


class SlotSignal:

    def __init__(self, sems):
        self.sems = sems

    def sem(self, b):
        return self.sems[b.slot]

    def landed(self, b):
        return self.sems[b.slot], (b.half + (b.passed // 2 + 1)) * 16

    def two_back(self, b):
        return self.sems[b.slot], (b.half + b.passed // 2) * 16


def gnn_program(nc, x, adj, w1, b1, w2, b2, wfc, afc, whand, ahand, wl1, al1, out):
    fp32 = mybir.dt.float32
    i32 = mybir.dt.int32
    ALU = mybir.AluOpType
    ACT = mybir.ActivationFunctionType
    AX = mybir.AxisListType

    B, N, D = x.shape
    H = w1.shape[1]
    C = N // P
    HT = H // P
    assert C == 4 and HT == 2 and D == P and w2.shape[1] == P and B % 4 == 0

    ctx = ExitStack()
    with ctx:
        def sb(name, shape, dt=fp32):
            return ctx.enter_context(nc.sbuf_tensor(name, shape, dt))

        def semaphore(name):
            return ctx.enter_context(nc.semaphore(name))

        ident = sb("ident", [P, P])
        minus_half = sb("minus_half", [P, C])
        minus_one = sb("minus_one", [P, 1])
        w1_sb = sb("w1_sb", [P, H])
        b1_sb = sb("b1_sb", [P, HT])
        w2_sb = sb("w2_sb", [P, HT, D])
        b2_sb = sb("b2_sb", [P, 1])
        wfc_sb = sb("wfc_sb", [P, HT, H + 2])
        whand_sb = sb("whand_sb", [P, 1, D + 2])
        wl1_sb = sb("wl1_sb", [P, 1, D + 2])
        afc_sb = sb("afc_sb", [P, 2, H])
        ahand_sb = sb("ahand_sb", [P, 2, D])
        al1_sb = sb("al1_sb", [P, 2, D])
        wa_tmp = sb("wa_tmp", [P, 2, H])
        adj_sb = sb("adj_sb", [P, C, N], i32)
        edge = sb("edge", [P, C, N])
        edge_or_empty = sb("edge_or_empty", [P, C, N])
        has_edge = sb("has_edge", [P, C])
        empty = sb("empty", [P, C])
        empty_arg = sb("empty_arg", [P, C])
        mask_t = sb("mask_t", [P, C, N])
        guard = sb("guard", [P, 2, C])
        guard_col = sb("guard_col", [P, 1])
        guard_all = sb("guard_all", [P, 1])
        guard_flag = sb("guard_flag", [P, 1], i32)

        x_in = sb("x_in", [P, 2, C, D])
        x_res = sb("x_res", [P, 2, C, D])
        stats = sb("stats", [P, 2, 2, C, 6])
        meanvar = sb("meanvar", [P, 2, 2, C, 2])
        var_eps = sb("var_eps", [P, 2, 2, C])
        rstd = sb("rstd", [P, 2, 2, C])
        shift = sb("shift", [P, 2, 2, C])
        normed = [sb(f"normed{k}", [P, 2, C, D]) for k in range(2)]
        normed_t = [sb(f"normed_t{k}", [P, 2, N]) for k in range(2)]
        o1_t = sb("o1_t", [P, 2, HT, N])
        z_t = sb("z_t", [P, 2, HT, N])
        o2_t = sb("o2_t", [P, 2, N])
        x1 = sb("x1", [P, 2, C, D])
        y_out = sb("y_out", [P, 2, C, D])

        class Layer:

            def __init__(self, k, width, w):
                self.k, self.width, self.w = k, width, w
                self.masked = k > 0
                self.ext = sb(f"ext{k}", [P, 2, C, width + 4])
                self.fmax_col = sb(f"fmax_col{k}", [P, 2, 1])
                self.fmax = sb(f"fmax{k}", [P, 2, 1])
                self.pos = sb(f"pos{k}", [P, 2, C])
                self.args = sb(f"args{k}", [P, 2, 3 * C])
                self.uvb = sb(f"uvb{k}", [P, 2, 3 * C])
                self.row = sb(f"row{k}", [P, 2, N])
                self.prob = sb(f"prob{k}", [P, 2, C, N])
                self.recip = sb(f"recip{k}", [P, 2, C])
                self.y = sb(f"y{k}", [P, C, width])
                self.neg = sb(f"neg{k}", [P, C, width])
                self.u = sb(f"u{k}", [P, C, width])
                self.scratch = nc.dram_tensor(f"row_scratch{k}", [2, N], fp32, kind="Internal").ap()

        gat1 = Layer(0, H, wfc_sb)
        gat2 = Layer(1, D, whand_sb)
        gat3 = Layer(2, D, wl1_sb)
        layers = [gat1, gat2, gat3]

        bound = edge_or_empty
        score = edge[:, 0:2]
        prob_n = edge[:, 2:4]
        lrelu = adj_sb[:, 0:2].bitcast(fp32)
        minus_max = sb("minus_max", [P, 2, 1])

        bank = [ctx.enter_context(nc.psum_tensor(f"bank{k}", [P, 512], fp32)) for k in range(8)]

        x_v = x.rearrange("b (p c) d -> b p c d", c=C)
        out_v = out.rearrange("b (p c) d -> b p c d", c=C)

        s_load = semaphore("weights_loaded")
        s_adj = semaphore("adj_loaded")
        s_pool = semaphore("pool_constants")
        s_wa = semaphore("wa_chain")
        s_mask = semaphore("mask_chain")
        s_mt = semaphore("mask_transposed")
        s_mc = semaphore("mask_copied")

        with nc.Block() as block:
            @block.sync
            def _(sp):
                sp.dma_start(adj_sb[:], adj.rearrange("(p c) j -> p c j", c=C)).then_inc(s_adj, 16)
                loads = [
                    (afc_sb[:], afc.rearrange("(t f) o -> o t f", t=2).broadcast_to([P, 2, H])),
                    (ahand_sb[:], ahand.rearrange("(t f) o -> o t f", t=2).broadcast_to([P, 2, D])),
                    (al1_sb[:], al1.rearrange("(t f) o -> o t f", t=2).broadcast_to([P, 2, D])),
                    (wfc_sb[:, :, 2:H + 2], wfc.rearrange("(k p) f -> p k f", p=P)),
                    (whand_sb[:, 0, 2:D + 2], whand),
                    (wl1_sb[:, 0, 2:D + 2], wl1),
                    (w1_sb[:], w1),
                    (w2_sb[:], w2.rearrange("(k p) f -> p k f", p=P)),
                    *((b1_sb[:, k:k + 1], b1[k * P:(k + 1) * P].rearrange("(p o) -> p o", o=1)) for k in range(HT)),
                    (b2_sb[:], b2.rearrange("(p o) -> p o", o=1)),
                ]
                for dst, src in loads:
                    sp.dma_start(dst, src).then_inc(s_load, 16)
                sp.wait_ge(s_load, 16 * len(loads))

            @block.gpsimd
            def _(pool):
                nc.gpsimd.memset(ident[:], 0.0).then_inc(s_pool, 1)
                pool.wait_ge(s_pool, 1)
                nc.gpsimd.affine_select(out=ident[:], in_=ident[:], compare_op=ALU.not_equal, fill=1.0, base=0,
                                        pattern=[[-1, P]], channel_multiplier=1).then_inc(s_pool, 1)
                nc.gpsimd.memset(minus_half[:], -0.5).then_inc(s_pool, 1)
                nc.gpsimd.memset(minus_one[:], -1.0).then_inc(s_pool, 1)
                nc.gpsimd.memset(guard[:], 0.0).then_inc(s_pool, 1)
                for L in layers:
                    nc.gpsimd.memset(L.ext[:, :, :, L.width + 2:L.width + 3], 1.0).then_inc(s_pool, 1)
                pool.wait_ge(s_pool, 8)

            @block.vector
            def _(dve):
                dve.wait_ge(s_load, 16 * (9 + HT))
                done = 0
                for a_sb, w_sb, kt, width in ((afc_sb, wfc_sb, HT, H), (ahand_sb, whand_sb, 1, D), (al1_sb, wl1_sb, 1, D)):
                    for k in range(kt):
                        for t in range(2):
                            if done:
                                dve.wait_ge(s_wa, done)
                            nc.vector.tensor_tensor(wa_tmp[:, t, 0:width], w_sb[:, k, 2:width + 2], a_sb[:, t, :],
                                                    ALU.mult).then_inc(s_wa, 1)
                            dve.wait_ge(s_wa, done + 1)
                            nc.vector.tensor_reduce(w_sb[:, k, t:t + 1], wa_tmp[:, t, 0:width], AX.X,
                                                    ALU.add).then_inc(s_wa, 1)
                            done += 2
                dve.wait_ge(s_adj, 16)
                nc.vector.tensor_scalar(edge[:], adj_sb[:], 0.0, None, ALU.is_gt).then_inc(s_mask, 1)
                dve.wait_ge(s_mask, 1)
                nc.vector.tensor_reduce(has_edge[:], edge[:], AX.X, ALU.max).then_inc(s_mask, 1)
                dve.wait_ge(s_mask, 2)
                nc.vector.tensor_scalar(empty[:], has_edge[:], -1.0, 1.0, ALU.mult, ALU.add).then_inc(s_mask, 1)
                dve.wait_ge(s_mask, 3)
                nc.vector.tensor_scalar(empty_arg[:], empty[:], EMPTY_ARG + 1e4, -1e4, ALU.mult,
                                        ALU.add).then_inc(s_mask, 1)
                for c in range(C):
                    nc.vector.tensor_scalar(edge_or_empty[:, c, :], edge[:, c, :], empty[:, c:c + 1], None,
                                            ALU.max).then_inc(s_mask, 1)
                for t in range(C):
                    dve.wait_ge(s_mt, t + 1)
                    nc.vector.tensor_copy(mask_t[:, t, :], bank[t][:]).then_inc(s_mc, 1)
                nc.vector.tensor_scalar(bound[:], edge[:], 1e38, MASKED, ALU.mult, ALU.add).then_inc(s_mask, 1)
                dve.wait_ge(s_mask, 4 + C + 1)

            @block.tensor
            def _(pe):
                pe.wait_ge(s_pool, 2)
                pe.wait_ge(s_mask, 4 + C)
                for t in range(C):
                    for c in range(C):
                        last = nc.tensor.transpose(bank[t][:, c * P:(c + 1) * P],
                                                   edge_or_empty[:, c, t:N:C], ident[:])
                    last.then_inc(s_mt, 1)

        def signal(name, per_batch, skipped=0):
            return Signal(semaphore(name), per_batch, skipped)

        def slots(name):
            return SlotSignal([semaphore(f"{name}{k}") for k in range(2)])

        waited = {name: semaphore(f"waited_{name}") for name in ("dve", "pool", "sp")}
        x_loaded = slots("x_loaded")
        xres_loaded = slots("xres_loaded")
        stored = slots("stored")
        stats_done = [signal(f"stats_done{k}", 4) for k in range(2)]
        aggr_done = [signal(f"aggr_done{k}", 4) for k in range(2)]
        var_ready = [signal(f"var_ready{k}", 1) for k in range(2)]
        rstd_ready = [signal(f"rstd_ready{k}", 1) for k in range(2)]
        shift_ready = [signal(f"shift_ready{k}", 1) for k in range(2)]
        normed_ready = [signal(f"normed_ready{k}", 4) for k in range(2)]
        norm_filled = [signal(f"norm_filled{k}", 1) for k in range(2)]
        norm_t_ready = [signal(f"norm_t_ready{k}", 1) for k in range(2)]
        o1_filled = signal("o1_filled", HT)
        o1_ready = signal("o1_ready", HT)
        z_filled = signal("z_filled", HT)
        z_ready = signal("z_ready", HT)
        o2_filled = signal("o2_filled", 1)
        o2_ready = signal("o2_ready", 1)
        o2n_filled = signal("o2n_filled", 1)
        v_ready = signal("v_ready", 1)
        x1_ready = signal("x1_ready", 1)
        y_ready = signal("y_ready", 1)

        class LayerSignals:
            def __init__(self, L):
                k = L.k
                parts = C if L is gat1 else C // 2
                self.h_filled = signal(f"h_filled{k}", parts)
                self.h_ready = signal(f"h_ready{k}", parts)
                self.fmax_col = signal(f"fmax_col{k}", 1)
                self.fmax = signal(f"fmax{k}", 1)
                self.pos = signal(f"pos{k}", 1)
                self.args = signal(f"args{k}", 3)
                self.guarded = signal(f"guarded{k}", 1)
                self.uvb = signal(f"uvb{k}", 1)
                self.row_written = slots(f"row_written{k}")
                self.row_loaded = slots(f"row_loaded{k}")
                self.unmasked = signal(f"unmasked{k}", C)
                self.prob_ready = signal(f"prob_ready{k}", C)
                self.g_filled = signal(f"g_filled{k}", parts)
                self.recip = signal(f"recip{k}", parts)
                self.g_ready = signal(f"g_ready{k}", C)
                self.neg = signal(f"neg{k}", 2 if L is gat1 else 1)
                self.exp = signal(f"exp{k}", 2 if L is gat1 else 1)
                self.exp2 = signal(f"exp2{k}", 2 if L is gat1 else 1)
                self.u = signal(f"u{k}", 2 if L is gat1 else 1)
                if L.masked:
                    self.bounded = signal(f"bounded{k}", C, B)
                    self.shifted = signal(f"shifted{k}", C, B)
                    self.lrelu = signal(f"lrelu{k}", C, B)
                    self.minus_max = signal(f"minus_max{k}", C, B)
                    self.prob_n = signal(f"prob_n{k}", C, B)
                    self.prob_filled = signal(f"prob_filled{k}", C, B)

        sig = {L: LayerSignals(L) for L in layers}
        s1, s2, s3 = (sig[L] for L in layers)

        def network(general, pipelined, passed):

            def where_needed(eng):
                return eng.If(eng.value_load(guard_flag[0:1, 0:1], min_val=0, max_val=1) > 0) if general else ExitStack()

            def factored(L):
                return not (general and L.masked)

            lock_step = ["load", "norm1a", "norm1b", "mlp1_turn", "mlp1", "h1", "max1", "args1", "prob1", "attend1a",
                         "attend1b", "elu1", "z", "mlp2", "h2", "max2", "args2", "prob2", "attend2", "elu2",
                         "norm2a", "norm2b", "turn2", "h3", "max3", "args3", "prob3", "attend3a", "attend3b", "elu3"]

            def run(eng, steps):

                def turn(half, slot, first, live):
                    for name, lag in order:
                        if live(lag) and name in steps:
                            r = slot - lag
                            steps[name](Batch(half + r // 2, r % 2, first - lag, passed))

                if not pipelined:
                    order = [(name, 0) for name in lock_step]
                    for t in range(2):
                        turn(0, t, t, lambda lag: True)
                    with eng.Fori(1, B // 2) as i:
                        for t in range(2):
                            turn(i, t, 2 + t, lambda lag: True)
                    return
                order = LAGGED
                deepest = max(lag for _, lag in order)
                for t in range(8):
                    turn(t // 2, t % 2, t, lambda lag: t >= lag)
                with eng.Fori(4, B // 2) as i:
                    for t in range(2):
                        turn(i, t, 8 + t, lambda lag: True)
                for t in range(B, B + deepest):
                    turn(t // 2, t % 2, t, lambda lag: t - lag < B)

            with nc.Block() as block:
                @block.sync
                def _(sp):
                    def load_x(b):
                        if b.first > 0:
                            sp.wait_ge(*normed_ready[0].two_back(b))
                        sp.dma_start(x_in[:, b.slot], x_v[b.n]).then_inc(x_loaded.sem(b), 16)

                    def load_x_again(b):
                        if b.first > 0:
                            sp.wait_ge(*x1_ready.two_back(b))
                        sp.dma_start(x_res[:, b.slot], x_v[b.n]).then_inc(xres_loaded.sem(b), 16)

                    def spread(b, L):
                        s = sig[L]
                        sp.wait_ge(*s.uvb.at(b, 1))
                        sp.sem_inc(waited["sp"], 1)
                        row = L.scratch[b.slot]
                        if b.first > 0:
                            sp.wait_ge(*s.row_loaded.two_back(b))
                        sp.dma_start(row.rearrange("(p c) -> p c", c=C),
                                     L.uvb[:, b.slot, 2 * C:3 * C]).then_inc(s.row_written.sem(b), 16)
                        sp.wait_ge(*s.row_written.landed(b))
                        sp.sem_inc(waited["sp"], 1)
                        if b.first > 0:
                            sp.wait_ge(*s.prob_ready.two_back(b))
                        sp.dma_start(L.row[:, b.slot],
                                     row.rearrange("(o n) -> o n", o=1).broadcast_to([P, N])).then_inc(
                            s.row_loaded.sem(b), 16)

                    def store(b):
                        sp.wait_ge(*y_ready.at(b, 1))
                        sp.dma_start(out_v[b.n], y_out[:, b.slot]).then_inc(stored.sem(b), 16)

                    steps = {
                        "load": load_x,
                        "args1": lambda b: spread(b, gat1),
                        "h2": load_x_again,
                        "args2": lambda b: spread(b, gat2),
                        "args3": lambda b: spread(b, gat3),
                        "elu3": store,
                    }
                    with where_needed(sp):
                        run(sp, steps)
                        for k in range(2):
                            sp.wait_ge(stored.sems[k], 16 * ((B + passed) // 2))

                @block.gpsimd
                def _(pool):
                    def root(b, k):
                        pool.wait_ge(*var_ready[k].at(b, 1))
                        nc.gpsimd.tensor_tensor(rstd[:, b.slot, k], var_eps[:, b.slot, k], minus_half[:],
                                                ALU.pow).then_inc(rstd_ready[k].sem, 1)

                    def maximum(b, L):
                        s = sig[L]
                        if factored(L):
                            pool.wait_ge(*s.fmax_col.at(b, 1))
                            if b.first > 0:
                                pool.wait_ge(*s.args.two_back(b))
                            pool.sem_inc(waited["pool"], 1)
                            nc.gpsimd.partition_all_reduce(L.fmax[:, b.slot], L.fmax_col[:, b.slot], P,
                                                           bass.bass_isa.ReduceOp.max).then_inc(s.fmax.sem, 1)

                    def result(b):
                        pool.wait_ge(*s3.u.at(b, 1))
                        pool.wait_ge(*x1_ready.at(b, 1))
                        if b.first > 0:
                            pool.wait_ge(*stored.two_back(b))
                        nc.gpsimd.tensor_tensor(y_out[:, b.slot], gat3.u[:], x1[:, b.slot], ALU.add).then_inc(
                            y_ready.sem, 1)

                    steps = {
                        "norm1a": lambda b: root(b, 0),
                        "norm2a": lambda b: root(b, 1),
                        "max1": lambda b: maximum(b, gat1),
                        "max2": lambda b: maximum(b, gat2),
                        "max3": lambda b: maximum(b, gat3),
                        "elu3": result,
                    }
                    with where_needed(pool):
                        run(pool, steps)

                @block.scalar
                def _(act):
                    def turned(b, k):
                        act.wait_ge(*norm_filled[k].at(b, 1))
                        if b.first > 0:
                            if k == 0:
                                act.wait_ge(*o1_filled.two_back(b))
                            else:
                                act.wait_ge(*s3.h_filled.two_back(b))
                        nc.scalar.activation(normed_t[k][:, b.slot], bank[6 * k][:], ACT.Copy).then_inc(
                            norm_t_ready[k].sem, 1)

                    def mlp1(b):
                        for f in range(HT):
                            act.wait_ge(*o1_filled.at(b, f + 1))
                            if b.first > 0 and f == 0:
                                act.wait_ge(*z_ready.two_back(b))
                                act.wait_ge(*s1.h_filled.two_back(b))
                            nc.scalar.activation(o1_t[:, b.slot, f], bank[1 - f][:], ACT.Relu,
                                                 bias=b1_sb[:, f:f + 1]).then_inc(o1_ready.sem, 1)

                    def h1(b):
                        for c in range(C):
                            act.wait_ge(*s1.h_filled.at(b, c + 1))
                            if b.first > 0 and c == 0:
                                act.wait_ge(*s1.g_filled.two_back(b))
                                act.wait_ge(*s1.args.two_back(b))
                            nc.scalar.activation(gat1.ext[:, b.slot, c, 0:H + 2], bank[(c + 1) % 2][:, 0:H + 2],
                                                 ACT.Copy).then_inc(s1.h_ready.sem, 1)

                    def h_masked(b, L, banks):
                        s = sig[L]
                        for q in range(C // 2):
                            act.wait_ge(*s.h_filled.at(b, q + 1))
                            if b.first > 0 and q == 0:
                                act.wait_ge(*s.g_filled.two_back(b))
                                if factored(L):
                                    act.wait_ge(*s.args.two_back(b))
                                else:
                                    act.wait_ge(*s.uvb.two_back(b))
                            if b.first > B and q == 0 and not factored(L):
                                act.wait_ge(*s.shifted.two_back(b))
                            nc.scalar.activation(
                                L.ext[:, b.slot, 2 * q:2 * q + 2, 0:D + 2],
                                banks[q][:, 0:2 * (D + 2)].rearrange("p (t n) -> p t n", t=2),
                                ACT.Copy).then_inc(s.h_ready.sem, 1)

                    def normalise(b, k, src):
                        act.wait_ge(*shift_ready[k].at(b, 1))
                        if b.first > 0:
                            act.wait_ge(*norm_filled[k].two_back(b))
                        for c in range(C):
                            nc.scalar.activation(normed[k][:, b.slot, c], src[:, c], ACT.Relu,
                                                 scale=rstd[:, b.slot, k, c:c + 1],
                                                 bias=shift[:, b.slot, k, c:c + 1]).then_inc(normed_ready[k].sem, 1)

                    def attended1(b, part):
                        for c in (2 * part, 2 * part + 1):
                            act.wait_ge(*s1.recip.at(b, c + 1))
                            act.wait_ge(*s1.u.before(b))
                            nc.scalar.activation(gat1.y[:, c], bank[2 + c % 2][:, 0:H], ACT.Copy,
                                                 scale=gat1.recip[:, b.slot, c:c + 1]).then_inc(s1.g_ready.sem, 1)

                    def attended_masked(b, L, banks, parts):
                        s = sig[L]
                        for q in parts:
                            act.wait_ge(*s.recip.at(b, q + 1))
                            act.wait_ge(*s.u.before(b))
                            for e in range(2):
                                c = 2 * q + e
                                nc.scalar.activation(L.y[:, c], banks[q][:, e * (D + 2):e * (D + 2) + D], ACT.Copy,
                                                     scale=L.recip[:, b.slot, c:c + 1]).then_inc(s.g_ready.sem, 1)

                    def h3(b):
                        h_masked(b, gat3, (bank[7], bank[6]))

                    def exponentials(b, L):
                        s = sig[L]
                        if factored(L):
                            act.wait_ge(*s.args.at(b, 3))
                            if b.first > 0:
                                act.wait_ge(*s.prob_ready.two_back(b))
                                act.wait_ge(*s.row_loaded.two_back(b))
                            nc.scalar.activation(L.uvb[:, b.slot], L.args[:, b.slot], ACT.Exp).then_inc(s.uvb.sem, 1)

                    def general_prob(b, L, banks):
                        s = sig[L]
                        for c in range(C):
                            act.wait_ge(*s.minus_max.at(b, c + 1))
                            if c >= 2:
                                act.wait_ge(*s.prob_filled.at(b, c - 1))
                            else:
                                act.wait_ge(*s.prob_filled.before(b))
                            nc.scalar.activation(prob_n[:, c % 2], lrelu[:, c % 2], ACT.Exp,
                                                 bias=minus_max[:, c % 2]).then_inc(s.prob_n.sem, 1)
                            act.wait_ge(*s.prob_filled.at(b, c + 1))
                            if b.first > 0:
                                act.wait_ge(*s.g_filled.two_back(b))
                            nc.scalar.activation(L.prob[:, b.slot, :, c * P:(c + 1) * P],
                                                 banks[c % 2][:].rearrange("p (t n) -> p t n", t=C),
                                                 ACT.Copy).then_inc(s.prob_ready.sem, 1)

                    def elu_twice(b, L, part, parts):
                        s = sig[L]
                        r = slice(part * C // parts, (part + 1) * C // parts)
                        act.wait_ge(*s.neg.at(b, part + 1))
                        nc.scalar.activation(L.neg[:, r], L.neg[:, r], ACT.Exp).then_inc(s.exp.sem, 1)
                        if L is gat3:
                            return
                        act.wait_ge(*s.exp.at(b, part + 1))
                        nc.scalar.activation(L.neg[:, r], L.neg[:, r], ACT.Exp, bias=minus_one[:]).then_inc(
                            s.exp2.sem, 1)

                    def mlp2(b):
                        act.wait_ge(*o2_filled.at(b, 1))
                        if b.first > 0:
                            act.wait_ge(*o2n_filled.two_back(b))
                        nc.scalar.activation(o2_t[:, b.slot], bank[2][:], ACT.Relu, bias=b2_sb[:]).then_inc(
                            o2_ready.sem, 1)

                    def attend1a(b):
                        attended1(b, 0)
                        elu_twice(b, gat1, 0, 2)

                    def attend1b(b):
                        attended1(b, 1)
                        elu_twice(b, gat1, 1, 2)

                    def attend2(b):
                        attended_masked(b, gat2, (bank[4], bank[5]), (0, 1))
                        elu_twice(b, gat2, 0, 1)

                    def attend3b(b):
                        attended_masked(b, gat3, (bank[7], bank[6]), (1,))
                        elu_twice(b, gat3, 0, 1)

                    steps = {
                        "mlp1": mlp1,
                        "h1": h1,
                        "norm1b": lambda b: normalise(b, 0, x_in[:, b.slot]),
                        "norm2b": lambda b: normalise(b, 1, x1[:, b.slot]),
                        "mlp1_turn": lambda b: turned(b, 0),
                        "turn2": lambda b: turned(b, 1),
                        "args1": lambda b: exponentials(b, gat1),
                        "attend1a": attend1a,
                        "attend1b": attend1b,
                        "mlp2": mlp2,
                        "h2": lambda b: h_masked(b, gat2, (bank[4], bank[5])),
                        "args2": lambda b: exponentials(b, gat2),
                        "prob2": (lambda b: general_prob(b, gat2, (bank[4], bank[5]))) if general else (lambda b: None),
                        "attend2": attend2,
                        "h3": h3,
                        "args3": lambda b: exponentials(b, gat3),
                        "prob3": (lambda b: general_prob(b, gat3, (bank[7], bank[6]))) if general else (lambda b: None),
                        "attend3a": lambda b: attended_masked(b, gat3, (bank[7], bank[6]), (0,)),
                        "attend3b": attend3b,
                    }
                    with where_needed(act):
                        run(act, steps)

                @block.vector
                def _(dve):
                    def moments(b, k, src):
                        st, mv = stats[:, b.slot, k], meanvar[:, b.slot, k]
                        for c in range(C):
                            nc.vector.bn_stats(st[:, c], src[:, c]).then_inc(stats_done[k].sem, 1)
                        dve.wait_ge(*stats_done[k].at(b, C))
                        dve.sem_inc(waited["dve"], 1)
                        for c in range(C):
                            nc.vector.bn_aggr(mv[:, c], st[:, c]).then_inc(aggr_done[k].sem, 1)
                        dve.wait_ge(*aggr_done[k].at(b, C))
                        nc.vector.tensor_scalar(var_eps[:, b.slot, k], mv[:, :, 1], LN_EPS, None, ALU.add).then_inc(
                            var_ready[k].sem, 1)

                    def mean_shift(b, k):
                        dve.wait_ge(*rstd_ready[k].at(b, 1))
                        nc.vector.scalar_tensor_tensor(out=shift[:, b.slot, k], in0=meanvar[:, b.slot, k, :, 0],
                                                       scalar=-1.0, in1=rstd[:, b.slot, k], op0=ALU.mult,
                                                       op1=ALU.mult).then_inc(shift_ready[k].sem, 1)

                    def norm1(b):
                        dve.wait_ge(*x_loaded.landed(b))
                        moments(b, 0, x_in[:, b.slot])

                    def maximum(b, L):
                        s = sig[L]
                        if factored(L):
                            dve.wait_ge(*s.h_ready.at(b, s.h_ready.per_batch))
                            nc.vector.tensor_reduce(L.fmax_col[:, b.slot], L.ext[:, b.slot, :, 1], AX.X,
                                                    ALU.max).then_inc(s.fmax_col.sem, 1)

                    def scores(b, L):
                        s = sig[L]
                        f1, f2 = L.ext[:, b.slot, :, 0], L.ext[:, b.slot, :, 1]
                        dve.wait_ge(*s.h_ready.at(b, s.h_ready.per_batch))
                        if not factored(L):
                            if b.first > 0:
                                dve.wait_ge(*s.row_loaded.two_back(b))
                            nc.vector.tensor_copy(L.uvb[:, b.slot, 2 * C:3 * C], f2).then_inc(s.uvb.sem, 1)
                            return
                        dve.wait_ge(*s.fmax.at(b, 1))
                        top = L.fmax[:, b.slot]
                        a = L.args[:, b.slot]
                        if b.first > 0:
                            dve.wait_ge(*s.uvb.two_back(b))
                        nc.vector.tensor_scalar(L.pos[:, b.slot], f1, top, 0.0, ALU.add, ALU.max).then_inc(s.pos.sem, 1)
                        nc.vector.tensor_scalar(a[:, 0:C], f2, top, None, ALU.subtract).then_inc(s.args.sem, 1)
                        nc.vector.tensor_scalar(a[:, C:2 * C], f2, top, SLOPE, ALU.subtract, ALU.mult).then_inc(
                            s.args.sem, 1)
                        dve.wait_ge(*s.pos.at(b, 1))
                        if L.masked:
                            nc.vector.scalar_tensor_tensor(out=a[:, 2 * C:3 * C], in0=L.pos[:, b.slot],
                                                           scalar=SLOPE - 1.0, in1=empty_arg[:], op0=ALU.mult,
                                                           op1=ALU.max).then_inc(s.args.sem, 1)
                            g = guard[:, L.k - 1]
                            dve.wait_ge(*s.args.at(b, 1))
                            dve.wait_ge(*s.guarded.before(b))
                            nc.vector.tensor_tensor(g, g, a[:, 0:C], ALU.min).then_inc(s.guarded.sem, 1)
                        else:
                            nc.vector.tensor_scalar(a[:, 2 * C:3 * C], L.pos[:, b.slot], SLOPE - 1.0, None,
                                                    ALU.mult).then_inc(s.args.sem, 1)

                    def prob(b, L):
                        s = sig[L]
                        p = L.prob[:, b.slot]
                        dve.wait_ge(*s.row_loaded.landed(b))
                        dve.wait_ge(*s.uvb.at(b, 1))
                        if b.first > 0:
                            dve.wait_ge(*s.g_filled.two_back(b))
                        row = L.row[:, b.slot].rearrange("q (p c) -> q c p", c=C)
                        for t in range(C):
                            nc.vector.tensor_scalar(
                                p[:, t].rearrange("q (c p) -> q c p", c=C), row,
                                L.uvb[:, b.slot, C + t:C + t + 1], L.uvb[:, b.slot, t:t + 1],
                                ALU.mult, ALU.max).then_inc((s.unmasked if L.masked else s.prob_ready).sem, 1)
                        if L.masked:
                            for t in range(C):
                                dve.wait_ge(*s.unmasked.at(b, t + 1))
                                nc.vector.tensor_tensor(p[:, t], p[:, t], mask_t[:, t], ALU.min).then_inc(
                                    s.prob_ready.sem, 1)

                    def general_prob(b, L):
                        s = sig[L]
                        dve.wait_ge(*s.row_loaded.landed(b))
                        dve.wait_ge(*s.h_ready.at(b, s.h_ready.per_batch))
                        for c in range(C):
                            if c >= 2:
                                dve.wait_ge(*s.prob_n.at(b, c - 1))
                            else:
                                dve.wait_ge(*s.prob_n.before(b))
                            nc.vector.tensor_tensor(score[:, c % 2], L.row[:, b.slot], bound[:, c],
                                                    ALU.min).then_inc(s.bounded.sem, 1)
                            dve.wait_ge(*s.bounded.at(b, c + 1))
                            nc.vector.tensor_scalar(score[:, c % 2], score[:, c % 2], L.ext[:, b.slot, c, 0:1], None,
                                                    ALU.add).then_inc(s.shifted.sem, 1)
                            dve.wait_ge(*s.shifted.at(b, c + 1))
                            nc.vector.scalar_tensor_tensor(out=lrelu[:, c % 2], in0=score[:, c % 2], scalar=SLOPE,
                                                           in1=score[:, c % 2], op0=ALU.mult, op1=ALU.max).then_inc(
                                s.lrelu.sem, 1)
                            dve.wait_ge(*s.lrelu.at(b, c + 1))
                            nc.vector.tensor_reduce(minus_max[:, c % 2], lrelu[:, c % 2], AX.X, ALU.max,
                                                    negate=True).then_inc(s.minus_max.sem, 1)

                    def prob_step(b, L):
                        if factored(L):
                            prob(b, L)
                        else:
                            general_prob(b, L)

                    def attend1(b, part):
                        s, L = s1, gat1
                        for c in (2 * part, 2 * part + 1):
                            dve.wait_ge(*s.g_filled.at(b, c + 1))
                            nc.vector.reciprocal(L.recip[:, b.slot, c:c + 1],
                                                 bank[2 + c % 2][:, H:H + 1]).then_inc(s.recip.sem, 1)
                        r = slice(2 * part, 2 * part + 2)
                        dve.wait_ge(*s.g_ready.at(b, 2 * part + 2))
                        nc.vector.tensor_scalar(L.neg[:, r], L.y[:, r], 0.0, None, ALU.min).then_inc(s.neg.sem, 1)

                    def elu(b, L, part, parts, used):
                        s = sig[L]
                        r = slice(part * C // parts, (part + 1) * C // parts)
                        dve.wait_ge(*(s.exp if L is gat3 else s.exp2).at(b, part + 1))
                        dve.wait_ge(*used.before(b))
                        nc.vector.scalar_tensor_tensor(out=L.u[:, r], in0=L.neg[:, r], scalar=-1.0, in1=L.y[:, r],
                                                       op0=ALU.add, op1=ALU.max).then_inc(s.u.sem, 1)

                    def attend1b(b):
                        attend1(b, 1)
                        elu(b, gat1, 0, 2, z_filled)

                    def residual1(b):
                        for f in range(HT):
                            dve.wait_ge(*z_filled.at(b, f + 1))
                            if b.first > 0 and f == 0:
                                dve.wait_ge(*o2_filled.two_back(b))
                            nc.vector.tensor_tensor(z_t[:, b.slot, f], bank[2 + f][:], o1_t[:, b.slot, f],
                                                    ALU.add).then_inc(z_ready.sem, 1)

                    def attend_masked(b, L, banks, parts):
                        s = sig[L]
                        for q in parts:
                            dve.wait_ge(*s.g_filled.at(b, q + 1))
                            ps = banks[q][:, 0:2 * (D + 2)].rearrange("p (t n) -> p t n", t=2)
                            nc.vector.reciprocal(L.recip[:, b.slot, 2 * q:2 * q + 2], ps[:, :, D]).then_inc(
                                s.recip.sem, 1)

                    def negatives(b, L):
                        s = sig[L]
                        dve.wait_ge(*s.g_ready.at(b, C))
                        nc.vector.tensor_scalar(L.neg[:], L.y[:], 0.0, None, ALU.min).then_inc(s.neg.sem, 1)

                    def attend2(b):
                        attend_masked(b, gat2, (bank[4], bank[5]), (0, 1))
                        negatives(b, gat2)

                    def attend3b(b):
                        attend_masked(b, gat3, (bank[7], bank[6]), (1,))
                        negatives(b, gat3)

                    def norm2(b):
                        dve.wait_ge(*s2.u.at(b, 1))
                        dve.wait_ge(*o2n_filled.at(b, 1))
                        v = gat2.u[:].rearrange("p c n -> p (c n)")
                        nc.vector.tensor_tensor(v, bank[4][:], v, ALU.add).then_inc(v_ready.sem, 1)
                        dve.wait_ge(*v_ready.at(b, 1))
                        dve.wait_ge(*xres_loaded.landed(b))
                        if b.first > 0:
                            dve.wait_ge(*y_ready.two_back(b))
                            dve.wait_ge(*normed_ready[1].two_back(b))
                        nc.vector.scalar_tensor_tensor(out=x1[:, b.slot], in0=gat2.u[:], scalar=0.0,
                                                       in1=x_res[:, b.slot], op0=ALU.max, op1=ALU.add).then_inc(
                            x1_ready.sem, 1)
                        dve.wait_ge(*x1_ready.at(b, 1))
                        moments(b, 1, x1[:, b.slot])

                    steps = {
                        "norm1a": norm1,
                        "norm1b": lambda b: mean_shift(b, 0),
                        "max1": lambda b: maximum(b, gat1),
                        "args1": lambda b: scores(b, gat1),
                        "prob1": lambda b: prob(b, gat1),
                        "attend1a": lambda b: attend1(b, 0),
                        "attend1b": attend1b,
                        "elu1": lambda b: elu(b, gat1, 1, 2, z_filled),
                        "z": residual1,
                        "max2": lambda b: maximum(b, gat2),
                        "args2": lambda b: scores(b, gat2),
                        "prob2": lambda b: prob_step(b, gat2),
                        "attend2": attend2,
                        "elu2": lambda b: elu(b, gat2, 0, 1, x1_ready),
                        "norm2a": norm2,
                        "norm2b": lambda b: mean_shift(b, 1),
                        "max3": lambda b: maximum(b, gat3),
                        "args3": lambda b: scores(b, gat3),
                        "prob3": lambda b: prob_step(b, gat3),
                        "attend3a": lambda b: attend_masked(b, gat3, (bank[7], bank[6]), (0,)),
                        "attend3b": attend3b,
                        "elu3": lambda b: elu(b, gat3, 0, 1, y_ready),
                    }
                    with where_needed(dve):
                        run(dve, steps)

                @block.tensor
                def _(pe):
                    def mlp1_turn(b):
                        pe.wait_ge(*normed_ready[0].at(b, C))
                        pe.wait_ge(*s1.h_ready.before(b))
                        for c in range(C):
                            last = nc.tensor.transpose(bank[0][:, c * P:(c + 1) * P], normed[0][:, b.slot, c],
                                                       ident[:])
                        last.then_inc(norm_filled[0].sem, 1)

                    def mlp1(b):
                        pe.wait_ge(*norm_t_ready[0].at(b, 1))
                        for f in range(HT):
                            nc.tensor.matmul(bank[1 - f][:], w1_sb[:, f * P:(f + 1) * P], normed_t[0][:, b.slot],
                                             start=True, stop=True).then_inc(o1_filled.sem, 1)

                    def h1(b):
                        pe.wait_ge(*o1_ready.at(b, HT))
                        for c in range(C):
                            if c >= 2:
                                pe.wait_ge(*s1.h_ready.at(b, c - 1))
                            for k in range(HT):
                                last = nc.tensor.matmul(bank[(c + 1) % 2][:, 0:H + 2],
                                                        o1_t[:, b.slot, k, c * P:(c + 1) * P], wfc_sb[:, k],
                                                        start=(k == 0), stop=(k == HT - 1))
                            last.then_inc(s1.h_filled.sem, 1)

                    def attend1(b, part):
                        for c in (2 * part, 2 * part + 1):
                            if c == 0:
                                pe.wait_ge(*o2_ready.before(b))
                                pe.wait_ge(*s1.h_ready.at(b, C))
                            elif c == 1:
                                pe.wait_ge(*z_ready.before(b))
                            else:
                                pe.wait_ge(*s1.g_ready.at(b, c - 1))
                            for t in range(C):
                                if c == 0:
                                    pe.wait_ge(*s1.prob_ready.at(b, t + 1))
                                last = nc.tensor.matmul(bank[2 + c % 2][:, 0:H + 1],
                                                        gat1.prob[:, b.slot, t, c * P:(c + 1) * P],
                                                        gat1.ext[:, b.slot, t, 2:H + 3],
                                                        start=(t == 0), stop=(t == C - 1))
                            last.then_inc(s1.g_filled.sem, 1)

                    def z(b):
                        pe.wait_ge(*s1.u.at(b, 2))
                        for f in range(HT):
                            pe.wait_ge(*s1.g_ready.at(b, 3 + f))
                            for c in range(C):
                                last = nc.tensor.transpose(bank[2 + f][:, c * P:(c + 1) * P],
                                                           gat1.u[:, c, f * P:(f + 1) * P], ident[:])
                            last.then_inc(z_filled.sem, 1)

                    def mlp2(b):
                        pe.wait_ge(*z_ready.at(b, HT))
                        for k in range(HT):
                            last = nc.tensor.matmul(bank[2][:], w2_sb[:, k], z_t[:, b.slot, k],
                                                    start=(k == 0), stop=(k == HT - 1))
                        last.then_inc(o2_filled.sem, 1)

                    def h_masked(b, L, src, banks):
                        s = sig[L]
                        for q in range(C // 2):
                            for e in range(2):
                                c = 2 * q + e
                                last = nc.tensor.matmul(banks[q][:, e * (D + 2):(e + 1) * (D + 2)],
                                                        src[:, c * P:(c + 1) * P], L.w[:, 0], start=True, stop=True)
                            last.then_inc(s.h_filled.sem, 1)

                    def h2(b):
                        pe.wait_ge(*o2_ready.at(b, 1))
                        pe.wait_ge(*v_ready.before(b))
                        pe.wait_ge(*s2.g_ready.before(b))
                        h_masked(b, gat2, o2_t[:, b.slot], (bank[4], bank[5]))

                    def turn2(b):
                        pe.wait_ge(*normed_ready[1].at(b, C))
                        pe.wait_ge(*s3.g_ready.before(b))
                        for c in range(C):
                            last = nc.tensor.transpose(bank[6][:, c * P:(c + 1) * P], normed[1][:, b.slot, c],
                                                       ident[:])
                        last.then_inc(norm_filled[1].sem, 1)

                    def h3(b):
                        pe.wait_ge(*norm_t_ready[1].at(b, 1))
                        h_masked(b, gat3, normed_t[1][:, b.slot], (bank[7], bank[6]))

                    def general_prob(b, L, banks):
                        s = sig[L]
                        for c in range(C):
                            pe.wait_ge(*s.prob_n.at(b, c + 1))
                            if c < 2:
                                pe.wait_ge(*s.h_ready.at(b, c + 1))
                            else:
                                pe.wait_ge(*s.prob_ready.at(b, c - 1))
                            for t in range(C):
                                last = nc.tensor.transpose(banks[c % 2][:, t * P:(t + 1) * P],
                                                           prob_n[:, c % 2, t:N:C], ident[:])
                            last.then_inc(s.prob_filled.sem, 1)

                    def attend_masked(b, L, banks, parts):
                        s = sig[L]
                        if 0 in parts:
                            pe.wait_ge(*s.h_ready.at(b, 2))
                            if not factored(L):
                                pe.wait_ge(*s.prob_ready.at(b, C))
                        for q in parts:
                            for e in range(2):
                                c = 2 * q + e
                                for t in range(C):
                                    if c == 0 and factored(L):
                                        pe.wait_ge(*s.prob_ready.at(b, t + 1))
                                    last = nc.tensor.matmul(banks[q][:, e * (D + 2):e * (D + 2) + D + 1],
                                                            L.prob[:, b.slot, t, c * P:(c + 1) * P],
                                                            L.ext[:, b.slot, t, 2:D + 3],
                                                            start=(t == 0), stop=(t == C - 1))
                            last.then_inc(s.g_filled.sem, 1)

                    def attend2(b):
                        attend_masked(b, gat2, (bank[4], bank[5]), (0, 1))

                    def elu2(b):
                        pe.wait_ge(*s2.g_ready.at(b, 2))
                        for c in range(C):
                            last = nc.tensor.transpose(bank[4][:, c * P:(c + 1) * P],
                                                       o2_t[:, b.slot, c * P:(c + 1) * P], ident[:])
                        last.then_inc(o2n_filled.sem, 1)

                    steps = {
                        "mlp1_turn": mlp1_turn,
                        "mlp1": mlp1,
                        "h1": h1,
                        "attend1a": lambda b: attend1(b, 0),
                        "attend1b": lambda b: attend1(b, 1),
                        "z": z,
                        "mlp2": mlp2,
                        "h2": h2,
                        "prob2": (lambda b: general_prob(b, gat2, (bank[4], bank[5]))) if general else (lambda b: None),
                        "attend2": attend2,
                        "elu2": elu2,
                        "turn2": turn2,
                        "h3": h3,
                        "prob3": (lambda b: general_prob(b, gat3, (bank[7], bank[6]))) if general else (lambda b: None),
                        "attend3a": lambda b: attend_masked(b, gat3, (bank[7], bank[6]), (0,)),
                        "attend3b": lambda b: attend_masked(b, gat3, (bank[7], bank[6]), (1,)),
                    }
                    with where_needed(pe):
                        run(pe, steps)

        network(general=False, pipelined=True, passed=0)

        s_guard = semaphore("guard_reduced")
        s_spread = semaphore("guard_over_partitions")
        s_flag = semaphore("guard_flag")

        with nc.Block() as block:
            @block.vector
            def _(dve):
                nc.vector.tensor_reduce(guard_col[:], guard[:], AX.XY, ALU.min, negate=True).then_inc(s_guard, 1)
                dve.wait_ge(s_spread, 1)
                nc.vector.tensor_scalar(guard_flag[:], guard_all[:], RANGE_LIMIT, None, ALU.is_gt).then_inc(s_flag, 1)
                dve.wait_ge(s_flag, 1)

            @block.gpsimd
            def _(pool):
                pool.wait_ge(s_guard, 1)
                nc.gpsimd.partition_all_reduce(guard_all[:], guard_col[:], P,
                                               bass.bass_isa.ReduceOp.max).then_inc(s_spread, 1)

        network(general=True, pipelined=False, passed=B)


_INS = ['x', 'adj', 'L0_gnn_mlp1_w', 'L0_gnn_mlp1_b', 'L0_gnn_mlp2_w', 'L0_gnn_mlp2_b', 'L0_gnn_W_fc', 'L0_gnn_a_fc',
        'L0_gnn_W_hand', 'L0_gnn_a_hand', 'L1_gnn_W', 'L1_gnn_a']
_OUTS = [((16, 512, 128), 'float32')]


def kernel(**inputs):
    import numpy as _np
    import concourse.bacc as _bacc
    from concourse import mybir as _mybir
    from concourse.bass_utils import run_bass_kernel_spmd as _run

    nc = _bacc.Bacc("TRN2", target_bir_lowering=False, num_devices=1)
    arrays, args = {}, []
    for name in _INS:
        a = _np.ascontiguousarray(inputs[name])
        arrays[f"in_{name}"] = a
        args.append(nc.dram_tensor(f"in_{name}", a.shape, _mybir.dt.from_np(a.dtype), kind="ExternalInput").ap())
    for i, (shape, dtype) in enumerate(_OUTS):
        dt = _mybir.dt.from_np(_np.dtype(dtype))
        args.append(nc.dram_tensor(f"out_{i}", shape, dt, kind="ExternalOutput").ap())
    gnn_program(nc, *args)
    r = _run(nc, [arrays], core_ids=[0])
    return r.results[0]["out_0"]
```

```python
import concourse.bass as bass
from concourse import mybir
from contextlib import ExitStack
import numpy as np

P = 128
SLOPE = 0.2
LN_EPS = 1e-5
MASKED = -9e15 / SLOPE
RANGE_LIMIT = 60.0
EMPTY_ARG = 69.0


LAGGED = {
    "sync": [
        ("load", 0), ("h2", 2), ("args2", 3), ("args3", 4), ("elu3", 5), ("args1", 1)
    ],
    "gpsimd": [
        ("norm2a", 4), ("max2", 3), ("norm1a", 0), ("max3", 4), ("max1", 1), ("elu3", 5)
    ],
    "scalar": [
        ("attend2b", 4), ("exp2", 4), ("mlp1", 1), ("attend3a", 5), ("mlp2", 3), ("h2", 3), ("attend3b", 5),
        ("norm2b", 4), ("args2", 3), ("turn2", 4), ("attend1a", 2), ("exp3", 5), ("h1a", 1), ("h3", 4),
        ("prob2a", 3), ("exp1a", 2), ("args3", 4), ("h1b", 1), ("above2", 3), ("norm1b", 0), ("prob3a", 4),
        ("attend1b", 2), ("args1", 1), ("mlp1_turn", 0), ("exp1b", 2), ("above3", 4), ("attend2a", 3)
    ],
    "vector": [
        ("prob3a", 5), ("attend2a", 4), ("elu1b", 3), ("attend2b", 4), ("prob3b", 5), ("exp2", 4), ("z", 3),
        ("attend3a", 5), ("elu2", 4), ("norm2a", 4), ("prob1", 2), ("attend3b", 5), ("norm2b", 4), ("max2", 3),
        ("exp3", 5), ("args2", 3), ("norm1a", 0), ("attend1a", 2), ("exp1a", 2), ("above2", 3), ("max3", 4),
        ("elu3", 5), ("args3", 4), ("prob2a", 3), ("norm1b", 0), ("max1", 1), ("prob2b", 3), ("args1", 1),
        ("attend1b", 2), ("elu1a", 2), ("above3", 4), ("exp1b", 2)
    ],
    "tensor": [
        ("prob3a", 5), ("prob2a", 4), ("attend2a", 4), ("mlp1_turn", 1), ("attend2b", 4), ("mlp1", 1), ("z", 3),
        ("attend3a", 5), ("turn_o2", 4), ("mlp2", 3), ("attend3b", 5), ("h2", 3), ("attend1a", 2), ("turn2", 4),
        ("h1a", 1), ("h3", 4), ("h1b", 1), ("attend1b", 2)
    ],
}


class Batch:

    def __init__(self, half, slot, first, passed):
        self.half, self.slot, self.first, self.passed = half, slot, first + passed, passed
        self.n = half * 2 + slot
        self.count = half * 2 + (slot + passed)


class Signal:

    def __init__(self, sem, per_batch, skipped=0):
        self.sem, self.per_batch, self.skipped = sem, per_batch, skipped

    def at(self, b, k):
        return self.sem, (b.count - self.skipped) * self.per_batch + k

    def before(self, b):
        return self.at(b, 0)

    def two_back(self, b):
        return self.at(b, -self.per_batch)


class SlotSignal:

    def __init__(self, sems):
        self.sems = sems

    def sem(self, b):
        return self.sems[b.slot]

    def landed(self, b):
        return self.sems[b.slot], (b.half + (b.passed // 2 + 1)) * 16

    def two_back(self, b):
        return self.sems[b.slot], (b.half + b.passed // 2) * 16


def gnn_program(nc, x, adj, w1, b1, w2, b2, wfc, afc, whand, ahand, wl1, al1, out):
    fp32 = mybir.dt.float32
    i32 = mybir.dt.int32
    ALU = mybir.AluOpType
    ACT = mybir.ActivationFunctionType
    AX = mybir.AxisListType

    B, N, D = x.shape
    H = w1.shape[1]
    C = N // P
    HT = H // P
    assert C == 4 and HT == 2 and D == P and w2.shape[1] == P and B % 4 == 0

    ctx = ExitStack()
    with ctx:
        def sb(name, shape, dt=fp32):
            return ctx.enter_context(nc.sbuf_tensor(name, shape, dt))

        def semaphore(name):
            return ctx.enter_context(nc.semaphore(name))

        ident = sb("ident", [P, P])
        minus_half = sb("minus_half", [P, C])
        minus_one = sb("minus_one", [P, 1])
        w1_sb = sb("w1_sb", [P, H])
        b1_sb = sb("b1_sb", [P, HT])
        w2_sb = sb("w2_sb", [P, HT, D])
        b2_sb = sb("b2_sb", [P, 1])
        wfc_sb = sb("wfc_sb", [P, HT, H + 2])
        whand_sb = sb("whand_sb", [P, 1, D + 2])
        wl1_sb = sb("wl1_sb", [P, 1, D + 2])
        afc_sb = sb("afc_sb", [P, 2, H])
        ahand_sb = sb("ahand_sb", [P, 2, D])
        al1_sb = sb("al1_sb", [P, 2, D])
        wa_tmp = sb("wa_tmp", [P, 2, H])
        adj_sb = sb("adj_sb", [P, C, N], i32)
        edge = sb("edge", [P, C, N])
        edge_or_empty = sb("edge_or_empty", [P, C, N])
        has_edge = sb("has_edge", [P, C])
        empty = sb("empty", [P, C])
        empty_arg = sb("empty_arg", [P, C])
        mask_t = sb("mask_t", [P, C, N])
        guard = sb("guard", [P, 2, C])
        guard_col = sb("guard_col", [P, 1])
        guard_all = sb("guard_all", [P, 1])
        guard_flag = sb("guard_flag", [P, 1], i32)

        x_in = sb("x_in", [P, 2, C, D])
        x_res = sb("x_res", [P, 2, C, D])
        stats = sb("stats", [P, 2, 2, C, 6])
        meanvar = sb("meanvar", [P, 2, 2, C, 2])
        var_eps = sb("var_eps", [P, 2, 2, C])
        rstd = sb("rstd", [P, 2, 2, C])
        shift = sb("shift", [P, 2, 2, C])
        normed = [sb(f"normed{k}", [P, 2, C, D]) for k in range(2)]
        normed_t = [sb(f"normed_t{k}", [P, 2, N]) for k in range(2)]
        o1_t = sb("o1_t", [P, 2, HT, N])
        z_t = sb("z_t", [P, 2, HT, N])
        o2_t = sb("o2_t", [P, 2, N])
        x1 = sb("x1", [P, 2, C, D])
        y_out = sb("y_out", [P, 2, C, D])

        class Layer:

            def __init__(self, k, width, w):
                self.k, self.width, self.w = k, width, w
                self.masked = k > 0
                self.ext = sb(f"ext{k}", [P, 2, C, width + 4])
                self.fmax_col = sb(f"fmax_col{k}", [P, 2, 1])
                self.fmax = sb(f"fmax{k}", [P, 2, 1])
                self.pos = sb(f"pos{k}", [P, 2, C])
                self.args = sb(f"args{k}", [P, 2, 3 * C])
                self.uvb = sb(f"uvb{k}", [P, 2, 3 * C])
                self.minus_u = sb(f"minus_u{k}", [P, 2, C])
                self.row = sb(f"row{k}", [P, 2, N])
                self.prob = sb(f"prob{k}", [P, 2, C, N])
                self.recip = sb(f"recip{k}", [P, 2, C])
                self.y = sb(f"y{k}", [P, C, width])
                self.neg = sb(f"neg{k}", [P, C, width])
                self.u = sb(f"u{k}", [P, C, width])
                self.scratch = nc.dram_tensor(f"row_scratch{k}", [2, N], fp32, kind="Internal").ap()

        gat1 = Layer(0, H, wfc_sb)
        gat2 = Layer(1, D, whand_sb)
        gat3 = Layer(2, D, wl1_sb)
        layers = [gat1, gat2, gat3]

        bound = edge_or_empty
        score = edge[:, 0:2]
        prob_n = edge[:, 2:4]
        lrelu = adj_sb[:, 0:2].bitcast(fp32)
        minus_max = sb("minus_max", [P, 2, 1])

        bank = [ctx.enter_context(nc.psum_tensor(f"bank{k}", [P, 512], fp32)) for k in range(8)]

        x_v = x.rearrange("b (p c) d -> b p c d", c=C)
        out_v = out.rearrange("b (p c) d -> b p c d", c=C)

        s_load = semaphore("weights_loaded")
        s_adj = semaphore("adj_loaded")
        s_pool = semaphore("pool_constants")
        s_wa = semaphore("wa_chain")
        s_mask = semaphore("mask_chain")
        s_mt = semaphore("mask_transposed")
        s_mc = semaphore("mask_copied")

        weights = [
            (w1_sb[:], w1),
            *((b1_sb[:, k:k + 1], b1[k * P:(k + 1) * P].rearrange("(p o) -> p o", o=1)) for k in range(HT)),
            (wfc_sb[:, :, 2:H + 2], wfc.rearrange("(k p) f -> p k f", p=P)),
            (afc_sb[:], afc.rearrange("(t f) o -> o t f", t=2).broadcast_to([P, 2, H])),
            (whand_sb[:, 0, 2:D + 2], whand),
            (ahand_sb[:], ahand.rearrange("(t f) o -> o t f", t=2).broadcast_to([P, 2, D])),
            (wl1_sb[:, 0, 2:D + 2], wl1),
            (al1_sb[:], al1.rearrange("(t f) o -> o t f", t=2).broadcast_to([P, 2, D])),
            (w2_sb[:], w2.rearrange("(k p) f -> p k f", p=P)),
            (b2_sb[:], b2.rearrange("(p o) -> p o", o=1)),
        ]
        WEIGHTS_LOADED = 16 * len(weights)
        POOL_CONSTANTS = 5 + 3
        WA_DONE = 2 * 2 * (HT + 1 + 1)

        def load_constants(act):
            for dst, src in weights:
                act.dma_start(dst, src).then_inc(s_load, 16)
            act.dma_start(adj_sb[:], adj.rearrange("(p c) j -> p c j", c=C)).then_inc(s_adj, 16)
            act.wait_ge(s_load, WEIGHTS_LOADED)
            act.wait_ge(s_pool, POOL_CONSTANTS)

        def pool_constants(pool):
            nc.gpsimd.memset(ident[:], 0.0).then_inc(s_pool, 1)
            pool.wait_ge(s_pool, 1)
            nc.gpsimd.affine_select(out=ident[:], in_=ident[:], compare_op=ALU.not_equal, fill=1.0, base=0,
                                    pattern=[[-1, P]], channel_multiplier=1).then_inc(s_pool, 1)
            nc.gpsimd.memset(minus_half[:], -0.5).then_inc(s_pool, 1)
            nc.gpsimd.memset(minus_one[:], -1.0).then_inc(s_pool, 1)
            nc.gpsimd.memset(guard[:], 0.0).then_inc(s_pool, 1)
            for L in layers:
                nc.gpsimd.memset(L.ext[:, :, :, L.width + 2:L.width + 3], 1.0).then_inc(s_pool, 1)
            pool.wait_ge(s_pool, POOL_CONSTANTS)

        def guard_ready(dve):
            dve.wait_ge(s_pool, POOL_CONSTANTS)

        def score_weights(dve):
            dve.wait_ge(s_load, WEIGHTS_LOADED)
            done = 0
            for a_sb, w_sb, kt, width in ((afc_sb, wfc_sb, HT, H), (ahand_sb, whand_sb, 1, D), (al1_sb, wl1_sb, 1, D)):
                for k in range(kt):
                    for t in range(2):
                        if done >= 4:
                            dve.wait_ge(s_wa, done - 2)
                        nc.vector.tensor_tensor(wa_tmp[:, t, 0:width], w_sb[:, k, 2:width + 2], a_sb[:, t, :],
                                                ALU.mult).then_inc(s_wa, 1)
                        dve.wait_ge(s_wa, done + 1)
                        nc.vector.tensor_reduce(w_sb[:, k, t:t + 1], wa_tmp[:, t, 0:width], AX.X,
                                                ALU.add).then_inc(s_wa, 1)
                        done += 2

        def masks(dve):
            dve.wait_ge(s_adj, 16)
            nc.vector.tensor_scalar(edge[:], adj_sb[:], 0.0, None, ALU.is_gt).then_inc(s_mask, 1)
            dve.wait_ge(s_mask, 1)
            nc.vector.tensor_reduce(has_edge[:], edge[:], AX.X, ALU.max).then_inc(s_mask, 1)
            dve.wait_ge(s_mask, 2)
            nc.vector.tensor_scalar(empty[:], has_edge[:], -1.0, 1.0, ALU.mult, ALU.add).then_inc(s_mask, 1)
            dve.wait_ge(s_mask, 3)
            nc.vector.tensor_scalar(empty_arg[:], empty[:], EMPTY_ARG + 1e4, -1e4, ALU.mult,
                                    ALU.add).then_inc(s_mask, 1)
            for c in range(C):
                nc.vector.tensor_scalar(edge_or_empty[:, c, :], edge[:, c, :], empty[:, c:c + 1], None,
                                        ALU.max).then_inc(s_mask, 1)

        def turned_masks(dve):
            for t in range(C):
                dve.wait_ge(s_mt, t + 1)
                nc.vector.tensor_copy(mask_t[:, t, :], bank[4 + t][:]).then_inc(s_mc, 1)
            nc.vector.tensor_scalar(bound[:], edge[:], 1e38, MASKED, ALU.mult, ALU.add).then_inc(s_mask, 1)
            dve.wait_ge(s_mc, C)
            dve.wait_ge(s_mask, 4 + C + 1)

        def turn_masks(pe):
            pe.wait_ge(s_mask, 4 + C)
            for t in range(C):
                for c in range(C):
                    last = nc.tensor.transpose(bank[4 + t][:, c * P:(c + 1) * P],
                                               edge_or_empty[:, c, t:N:C], ident[:])
                last.then_inc(s_mt, 1)
            pe.wait_ge(s_mc, C)

        def weights_ready(pe):
            pe.wait_ge(s_pool, POOL_CONSTANTS)
            pe.wait_ge(s_load, WEIGHTS_LOADED)

        def score_weights_ready(pe):
            pe.wait_ge(s_wa, WA_DONE)

        def signal(name, per_batch, skipped=0):
            return Signal(semaphore(name), per_batch, skipped)

        def slots(name):
            return SlotSignal([semaphore(f"{name}{k}") for k in range(2)])

        waited = {name: semaphore(f"waited_{name}") for name in ("dve", "pool", "sp")}
        x_loaded = slots("x_loaded")
        xres_loaded = slots("xres_loaded")
        stored = slots("stored")
        stats_done = [signal(f"stats_done{k}", 4) for k in range(2)]
        aggr_done = [signal(f"aggr_done{k}", 4) for k in range(2)]
        var_ready = [signal(f"var_ready{k}", 1) for k in range(2)]
        rstd_ready = [signal(f"rstd_ready{k}", 1) for k in range(2)]
        shift_ready = [signal(f"shift_ready{k}", 1) for k in range(2)]
        normed_ready = [signal(f"normed_ready{k}", 4) for k in range(2)]
        norm_filled = [signal(f"norm_filled{k}", 1) for k in range(2)]
        norm_t_ready = [signal(f"norm_t_ready{k}", 1) for k in range(2)]
        o1_filled = signal("o1_filled", HT)
        o1_ready = signal("o1_ready", HT)
        z_filled = signal("z_filled", HT)
        z_ready = signal("z_ready", HT)
        o2_filled = signal("o2_filled", 1)
        o2_ready = signal("o2_ready", 1)
        o2n_filled = signal("o2n_filled", 1)
        v_ready = signal("v_ready", 1)
        x1_ready = signal("x1_ready", 1)
        y_ready = signal("y_ready", 1)

        class LayerSignals:
            def __init__(self, L):
                k = L.k
                parts = C if L is gat1 else C // 2
                self.h_filled = signal(f"h_filled{k}", parts)
                self.h_ready = signal(f"h_ready{k}", parts)
                self.fmax_col = signal(f"fmax_col{k}", 1)
                self.fmax = signal(f"fmax{k}", 1)
                self.pos = signal(f"pos{k}", 1)
                self.args = signal(f"args{k}", 3)
                self.guarded = signal(f"guarded{k}", 1)
                self.uvb = signal(f"uvb{k}", 1)
                self.row_written = slots(f"row_written{k}")
                self.row_loaded = slots(f"row_loaded{k}")
                self.unmasked = signal(f"unmasked{k}", C // 2)
                self.minus_u = signal(f"minus_u{k}", 1)
                self.above_u = signal(f"above_u{k}", C // 2)
                self.prob_ready = signal(f"prob_ready{k}", C)
                self.g_filled = signal(f"g_filled{k}", parts)
                self.recip = signal(f"recip{k}", parts)
                self.g_ready = signal(f"g_ready{k}", C)
                self.neg = signal(f"neg{k}", 2 if L is gat1 else 1)
                self.exp = signal(f"exp{k}", 2 if L is gat1 else 1)
                self.exp2 = signal(f"exp2{k}", 2 if L is gat1 else 1)
                self.u = signal(f"u{k}", 2 if L is gat1 else 1)
                if L.masked:
                    self.bounded = signal(f"bounded{k}", C, B)
                    self.shifted = signal(f"shifted{k}", C, B)
                    self.lrelu = signal(f"lrelu{k}", C, B)
                    self.minus_max = signal(f"minus_max{k}", C, B)
                    self.prob_n = signal(f"prob_n{k}", C, B)
                    self.prob_filled = signal(f"prob_filled{k}", C, B)

        sig = {L: LayerSignals(L) for L in layers}
        s1, s2, s3 = (sig[L] for L in layers)

        def network(general, pipelined, passed):

            def where_needed(eng):
                return eng.If(eng.value_load(guard_flag[0:1, 0:1], min_val=0, max_val=1) > 0) if general else ExitStack()

            def factored(L):
                return not (general and L.masked)

            lock_step = ["load", "norm1a", "norm1b", "mlp1_turn", "mlp1", "h1a", "h1b", "max1", "args1", "prob1",
                         "attend1a", "exp1a", "attend1b", "exp1b", "elu1a", "elu1b", "z", "mlp2", "h2", "max2",
                         "args2", "above2", "prob2a", "prob2b", "attend2a", "attend2b", "exp2", "turn_o2", "elu2",
                         "norm2a", "norm2b", "turn2", "h3", "max3", "args3", "above3", "prob3a", "prob3b",
                         "attend3a", "attend3b", "exp3", "elu3"]

            def run(eng, steps, lagged, before_turn={}):

                def turn(half, slot, first, live):
                    for name, lag in order:
                        if live(lag) and name in steps:
                            r = slot - lag
                            steps[name](Batch(half + r // 2, r % 2, first - lag, passed))

                if not pipelined:
                    order = [(name, 0) for name in lock_step]
                    for t in range(2):
                        turn(0, t, t, lambda lag: True)
                    with eng.Fori(1, B // 2) as i:
                        for t in range(2):
                            turn(i, t, 2 + t, lambda lag: True)
                    return
                order = lagged
                deepest = max(lag for _, lag in order)
                for t in range(8):
                    if t in before_turn:
                        before_turn[t](eng)
                    turn(t // 2, t % 2, t, lambda lag: t >= lag)
                with eng.Fori(4, B // 2) as i:
                    for t in range(2):
                        turn(i, t, 8 + t, lambda lag: True)
                for t in range(B, B + deepest):
                    turn(t // 2, t % 2, t, lambda lag: t - lag < B)

            with nc.Block() as block:
                @block.sync
                def _(sp):
                    def load_x(b):
                        if b.first > 0:
                            sp.wait_ge(*normed_ready[0].two_back(b))
                        sp.dma_start(x_in[:, b.slot], x_v[b.n]).then_inc(x_loaded.sem(b), 16)

                    def load_x_again(b):
                        if b.first > 0:
                            sp.wait_ge(*x1_ready.two_back(b))
                        sp.dma_start(x_res[:, b.slot], x_v[b.n]).then_inc(xres_loaded.sem(b), 16)

                    def spread(b, L):
                        s = sig[L]
                        sp.wait_ge(*s.uvb.at(b, 1))
                        sp.sem_inc(waited["sp"], 1)
                        row = L.scratch[b.slot]
                        if b.first > 0:
                            sp.wait_ge(*s.row_loaded.two_back(b))
                        sp.dma_start(row.rearrange("(p c) -> p c", c=C),
                                     L.uvb[:, b.slot, 2 * C:3 * C]).then_inc(s.row_written.sem(b), 16)
                        sp.wait_ge(*s.row_written.landed(b))
                        sp.sem_inc(waited["sp"], 1)
                        if b.first > 0:
                            sp.wait_ge(*s.prob_ready.two_back(b))
                        sp.dma_start(L.row[:, b.slot],
                                     row.rearrange("(o n) -> o n", o=1).broadcast_to([P, N])).then_inc(
                            s.row_loaded.sem(b), 16)

                    def store(b):
                        sp.wait_ge(*y_ready.at(b, 1))
                        sp.dma_start(out_v[b.n], y_out[:, b.slot]).then_inc(stored.sem(b), 16)

                    steps = {
                        "load": load_x,
                        "args1": lambda b: spread(b, gat1),
                        "h2": load_x_again,
                        "args2": lambda b: spread(b, gat2),
                        "args3": lambda b: spread(b, gat3),
                        "elu3": store,
                    }
                    with where_needed(sp):
                        run(sp, steps, LAGGED["sync"])
                        for k in range(2):
                            sp.wait_ge(stored.sems[k], 16 * ((B + passed) // 2))

                @block.gpsimd
                def _(pool):
                    def root(b, k):
                        pool.wait_ge(*var_ready[k].at(b, 1))
                        nc.gpsimd.tensor_tensor(rstd[:, b.slot, k], var_eps[:, b.slot, k], minus_half[:],
                                                ALU.pow).then_inc(rstd_ready[k].sem, 1)

                    def maximum(b, L):
                        s = sig[L]
                        if factored(L):
                            pool.wait_ge(*s.fmax_col.at(b, 1))
                            if b.first > 0:
                                pool.wait_ge(*s.args.two_back(b))
                            pool.sem_inc(waited["pool"], 1)
                            nc.gpsimd.partition_all_reduce(L.fmax[:, b.slot], L.fmax_col[:, b.slot], P,
                                                           bass.bass_isa.ReduceOp.max).then_inc(s.fmax.sem, 1)

                    def result(b):
                        pool.wait_ge(*s3.u.at(b, 1))
                        pool.wait_ge(*x1_ready.at(b, 1))
                        if b.first > 0:
                            pool.wait_ge(*stored.two_back(b))
                        nc.gpsimd.tensor_tensor(y_out[:, b.slot], gat3.u[:], x1[:, b.slot], ALU.add).then_inc(
                            y_ready.sem, 1)

                    steps = {
                        "norm1a": lambda b: root(b, 0),
                        "norm2a": lambda b: root(b, 1),
                        "max1": lambda b: maximum(b, gat1),
                        "max2": lambda b: maximum(b, gat2),
                        "max3": lambda b: maximum(b, gat3),
                        "elu3": result,
                    }
                    with where_needed(pool):
                        run(pool, steps, LAGGED["gpsimd"], {0: pool_constants})

                @block.scalar
                def _(act):
                    def turned(b, k):
                        act.wait_ge(*norm_filled[k].at(b, 1))
                        if b.first > 0:
                            if k == 0:
                                act.wait_ge(*o1_filled.two_back(b))
                            else:
                                act.wait_ge(*s3.h_filled.two_back(b))
                        nc.scalar.activation(normed_t[k][:, b.slot], bank[6 * k][:], ACT.Copy).then_inc(
                            norm_t_ready[k].sem, 1)

                    def mlp1(b):
                        for f in range(HT):
                            act.wait_ge(*o1_filled.at(b, f + 1))
                            if b.first > 0 and f == 0:
                                act.wait_ge(*z_ready.two_back(b))
                                act.wait_ge(*s1.h_filled.two_back(b))
                            nc.scalar.activation(o1_t[:, b.slot, f], bank[1 - f][:], ACT.Relu,
                                                 bias=b1_sb[:, f:f + 1]).then_inc(o1_ready.sem, 1)

                    def h1(b, part):
                        for c in (2 * part, 2 * part + 1):
                            act.wait_ge(*s1.h_filled.at(b, c + 1))
                            if b.first > 0 and c == 0:
                                act.wait_ge(*s1.g_filled.two_back(b))
                                act.wait_ge(*s1.args.two_back(b))
                            nc.scalar.activation(gat1.ext[:, b.slot, c, 0:H + 2], bank[(c + 1) % 2][:, 0:H + 2],
                                                 ACT.Copy).then_inc(s1.h_ready.sem, 1)

                    def h_masked(b, L, banks):
                        s = sig[L]
                        for q in range(C // 2):
                            act.wait_ge(*s.h_filled.at(b, q + 1))
                            if b.first > 0 and q == 0:
                                act.wait_ge(*s.g_filled.two_back(b))
                                if factored(L):
                                    act.wait_ge(*s.args.two_back(b))
                                else:
                                    act.wait_ge(*s.uvb.two_back(b))
                            if b.first > B and q == 0 and not factored(L):
                                act.wait_ge(*s.shifted.two_back(b))
                            nc.scalar.activation(
                                L.ext[:, b.slot, 2 * q:2 * q + 2, 0:D + 2],
                                banks[q][:, 0:2 * (D + 2)].rearrange("p (t n) -> p t n", t=2),
                                ACT.Copy).then_inc(s.h_ready.sem, 1)

                    def normalise(b, k, src):
                        act.wait_ge(*shift_ready[k].at(b, 1))
                        if b.first > 0:
                            act.wait_ge(*norm_filled[k].two_back(b))
                        for c in range(C):
                            nc.scalar.activation(normed[k][:, b.slot, c], src[:, c], ACT.Relu,
                                                 scale=rstd[:, b.slot, k, c:c + 1],
                                                 bias=shift[:, b.slot, k, c:c + 1]).then_inc(normed_ready[k].sem, 1)

                    def attended1(b, part):
                        for c in (2 * part, 2 * part + 1):
                            act.wait_ge(*s1.recip.at(b, c + 1))
                            act.wait_ge(*s1.u.before(b))
                            nc.scalar.activation(gat1.y[:, c], bank[2 + c % 2][:, 0:H], ACT.Copy,
                                                 scale=gat1.recip[:, b.slot, c:c + 1]).then_inc(s1.g_ready.sem, 1)

                    def attended_masked(b, L, banks, parts):
                        s = sig[L]
                        for q in parts:
                            act.wait_ge(*s.recip.at(b, q + 1))
                            act.wait_ge(*s.u.before(b))
                            for e in range(2):
                                c = 2 * q + e
                                nc.scalar.activation(L.y[:, c], banks[q][:, e * (D + 2):e * (D + 2) + D], ACT.Copy,
                                                     scale=L.recip[:, b.slot, c:c + 1]).then_inc(s.g_ready.sem, 1)

                    def h3(b):
                        h_masked(b, gat3, (bank[7], bank[6]))

                    def exponentials(b, L):
                        s = sig[L]
                        if factored(L):
                            act.wait_ge(*s.args.at(b, 3))
                            if b.first > 0:
                                act.wait_ge(*s.prob_ready.two_back(b))
                                act.wait_ge(*s.row_loaded.two_back(b))
                            nc.scalar.activation(L.uvb[:, b.slot], L.args[:, b.slot], ACT.Exp).then_inc(s.uvb.sem, 1)

                    def above_u(b, L):
                        s = sig[L]
                        act.wait_ge(*s.minus_u.at(b, 1))
                        act.wait_ge(*s.row_loaded.landed(b))
                        if b.first > 0:
                            act.wait_ge(*s.g_filled.two_back(b))
                        row = L.row[:, b.slot].rearrange("q (p c) -> q c p", c=C)
                        for t in range(C // 2, C):
                            nc.scalar.activation(
                                L.prob[:, b.slot, t].rearrange("q (c p) -> q c p", c=C), row, ACT.Relu,
                                scale=L.uvb[:, b.slot, C + t:C + t + 1],
                                bias=L.minus_u[:, b.slot, t:t + 1]).then_inc(s.above_u.sem, 1)

                    def general_prob(b, L, banks):
                        s = sig[L]
                        for c in range(C):
                            act.wait_ge(*s.minus_max.at(b, c + 1))
                            if c >= 2:
                                act.wait_ge(*s.prob_filled.at(b, c - 1))
                            else:
                                act.wait_ge(*s.prob_filled.before(b))
                            nc.scalar.activation(prob_n[:, c % 2], lrelu[:, c % 2], ACT.Exp,
                                                 bias=minus_max[:, c % 2]).then_inc(s.prob_n.sem, 1)
                            act.wait_ge(*s.prob_filled.at(b, c + 1))
                            if b.first > 0:
                                act.wait_ge(*s.g_filled.two_back(b))
                            nc.scalar.activation(L.prob[:, b.slot, :, c * P:(c + 1) * P],
                                                 banks[c % 2][:].rearrange("p (t n) -> p t n", t=C),
                                                 ACT.Copy).then_inc(s.prob_ready.sem, 1)

                    def elu_twice(b, L, part, parts):
                        s = sig[L]
                        r = slice(part * C // parts, (part + 1) * C // parts)
                        act.wait_ge(*s.neg.at(b, part + 1))
                        nc.scalar.activation(L.neg[:, r], L.neg[:, r], ACT.Exp).then_inc(s.exp.sem, 1)
                        if L is gat3:
                            return
                        act.wait_ge(*s.exp.at(b, part + 1))
                        nc.scalar.activation(L.neg[:, r], L.neg[:, r], ACT.Exp, bias=minus_one[:]).then_inc(
                            s.exp2.sem, 1)

                    def mlp2(b):
                        act.wait_ge(*o2_filled.at(b, 1))
                        if b.first > 0:
                            act.wait_ge(*o2n_filled.two_back(b))
                        nc.scalar.activation(o2_t[:, b.slot], bank[2][:], ACT.Relu, bias=b2_sb[:]).then_inc(
                            o2_ready.sem, 1)

                    steps = {
                        "mlp1": mlp1,
                        "h1a": lambda b: h1(b, 0),
                        "h1b": lambda b: h1(b, 1),
                        "norm1b": lambda b: normalise(b, 0, x_in[:, b.slot]),
                        "norm2b": lambda b: normalise(b, 1, x1[:, b.slot]),
                        "mlp1_turn": lambda b: turned(b, 0),
                        "turn2": lambda b: turned(b, 1),
                        "args1": lambda b: exponentials(b, gat1),
                        "attend1a": lambda b: attended1(b, 0),
                        "attend1b": lambda b: attended1(b, 1),
                        "exp1a": lambda b: elu_twice(b, gat1, 0, 2),
                        "exp1b": lambda b: elu_twice(b, gat1, 1, 2),
                        "mlp2": mlp2,
                        "h2": lambda b: h_masked(b, gat2, (bank[4], bank[5])),
                        "args2": lambda b: exponentials(b, gat2),
                        "prob2a": (lambda b: general_prob(b, gat2, (bank[4], bank[5]))) if general else (lambda b: None),
                        "above2": (lambda b: None) if general else (lambda b: above_u(b, gat2)),
                        "attend2a": lambda b: attended_masked(b, gat2, (bank[4], bank[5]), (0,)),
                        "attend2b": lambda b: attended_masked(b, gat2, (bank[4], bank[5]), (1,)),
                        "exp2": lambda b: elu_twice(b, gat2, 0, 1),
                        "h3": h3,
                        "args3": lambda b: exponentials(b, gat3),
                        "prob3a": (lambda b: general_prob(b, gat3, (bank[7], bank[6]))) if general else (lambda b: None),
                        "above3": (lambda b: None) if general else (lambda b: above_u(b, gat3)),
                        "attend3a": lambda b: attended_masked(b, gat3, (bank[7], bank[6]), (0,)),
                        "attend3b": lambda b: attended_masked(b, gat3, (bank[7], bank[6]), (1,)),
                        "exp3": lambda b: elu_twice(b, gat3, 0, 1),
                    }
                    with where_needed(act):
                        run(act, steps, LAGGED["scalar"], {0: load_constants})

                @block.vector
                def _(dve):
                    def moments(b, k, src):
                        st, mv = stats[:, b.slot, k], meanvar[:, b.slot, k]
                        for c in range(C):
                            nc.vector.bn_stats(st[:, c], src[:, c]).then_inc(stats_done[k].sem, 1)
                        dve.wait_ge(*stats_done[k].at(b, C))
                        dve.sem_inc(waited["dve"], 1)
                        for c in range(C):
                            nc.vector.bn_aggr(mv[:, c], st[:, c]).then_inc(aggr_done[k].sem, 1)
                        dve.wait_ge(*aggr_done[k].at(b, C))
                        nc.vector.tensor_scalar(var_eps[:, b.slot, k], mv[:, :, 1], LN_EPS, None, ALU.add).then_inc(
                            var_ready[k].sem, 1)

                    def mean_shift(b, k):
                        dve.wait_ge(*rstd_ready[k].at(b, 1))
                        nc.vector.scalar_tensor_tensor(out=shift[:, b.slot, k], in0=meanvar[:, b.slot, k, :, 0],
                                                       scalar=-1.0, in1=rstd[:, b.slot, k], op0=ALU.mult,
                                                       op1=ALU.mult).then_inc(shift_ready[k].sem, 1)

                    def norm1(b):
                        dve.wait_ge(*x_loaded.landed(b))
                        moments(b, 0, x_in[:, b.slot])

                    def maximum(b, L):
                        s = sig[L]
                        if factored(L):
                            dve.wait_ge(*s.h_ready.at(b, s.h_ready.per_batch))
                            nc.vector.tensor_reduce(L.fmax_col[:, b.slot], L.ext[:, b.slot, :, 1], AX.X,
                                                    ALU.max).then_inc(s.fmax_col.sem, 1)

                    def scores(b, L):
                        s = sig[L]
                        f1, f2 = L.ext[:, b.slot, :, 0], L.ext[:, b.slot, :, 1]
                        dve.wait_ge(*s.h_ready.at(b, s.h_ready.per_batch))
                        if not factored(L):
                            if b.first > 0:
                                dve.wait_ge(*s.row_loaded.two_back(b))
                            nc.vector.tensor_copy(L.uvb[:, b.slot, 2 * C:3 * C], f2).then_inc(s.uvb.sem, 1)
                            return
                        dve.wait_ge(*s.fmax.at(b, 1))
                        top = L.fmax[:, b.slot]
                        a = L.args[:, b.slot]
                        if b.first > 0:
                            dve.wait_ge(*s.uvb.two_back(b))
                        nc.vector.tensor_scalar(L.pos[:, b.slot], f1, top, 0.0, ALU.add, ALU.max).then_inc(s.pos.sem, 1)
                        nc.vector.tensor_scalar(a[:, 0:C], f2, top, None, ALU.subtract).then_inc(s.args.sem, 1)
                        nc.vector.tensor_scalar(a[:, C:2 * C], f2, top, SLOPE, ALU.subtract, ALU.mult).then_inc(
                            s.args.sem, 1)
                        dve.wait_ge(*s.pos.at(b, 1))
                        if L.masked:
                            nc.vector.scalar_tensor_tensor(out=a[:, 2 * C:3 * C], in0=L.pos[:, b.slot],
                                                           scalar=SLOPE - 1.0, in1=empty_arg[:], op0=ALU.mult,
                                                           op1=ALU.max).then_inc(s.args.sem, 1)
                            g = guard[:, L.k - 1]
                            dve.wait_ge(*s.args.at(b, 1))
                            dve.wait_ge(*s.guarded.before(b))
                            nc.vector.tensor_tensor(g, g, a[:, 0:C], ALU.min).then_inc(s.guarded.sem, 1)
                        else:
                            nc.vector.tensor_scalar(a[:, 2 * C:3 * C], L.pos[:, b.slot], SLOPE - 1.0, None,
                                                    ALU.mult).then_inc(s.args.sem, 1)

                    def prob(b, L, part):
                        s = sig[L]
                        p = L.prob[:, b.slot]
                        dve.wait_ge(*s.row_loaded.landed(b))
                        dve.wait_ge(*s.uvb.at(b, 1))
                        if b.first > 0:
                            dve.wait_ge(*s.g_filled.two_back(b))
                        tiles = (2 * part, 2 * part + 1)
                        if L.masked and part == 1:
                            for t in tiles:
                                dve.wait_ge(*s.above_u.at(b, t - C // 2 + 1))
                                nc.vector.scalar_tensor_tensor(out=p[:, t], in0=p[:, t],
                                                               scalar=L.uvb[:, b.slot, t:t + 1], in1=mask_t[:, t],
                                                               op0=ALU.add, op1=ALU.min).then_inc(
                                    s.prob_ready.sem, 1)
                            return
                        row = L.row[:, b.slot].rearrange("q (p c) -> q c p", c=C)
                        for t in tiles:
                            nc.vector.tensor_scalar(
                                p[:, t].rearrange("q (c p) -> q c p", c=C), row,
                                L.uvb[:, b.slot, C + t:C + t + 1], L.uvb[:, b.slot, t:t + 1],
                                ALU.mult, ALU.max).then_inc((s.unmasked if L.masked else s.prob_ready).sem, 1)
                        if L.masked:
                            for t in tiles:
                                dve.wait_ge(*s.unmasked.at(b, t + 1))
                                nc.vector.tensor_tensor(p[:, t], p[:, t], mask_t[:, t], ALU.min).then_inc(
                                    s.prob_ready.sem, 1)

                    def general_prob(b, L):
                        s = sig[L]
                        dve.wait_ge(*s.row_loaded.landed(b))
                        dve.wait_ge(*s.h_ready.at(b, s.h_ready.per_batch))
                        for c in range(C):
                            if c >= 2:
                                dve.wait_ge(*s.prob_n.at(b, c - 1))
                            else:
                                dve.wait_ge(*s.prob_n.before(b))
                            nc.vector.tensor_tensor(score[:, c % 2], L.row[:, b.slot], bound[:, c],
                                                    ALU.min).then_inc(s.bounded.sem, 1)
                            dve.wait_ge(*s.bounded.at(b, c + 1))
                            nc.vector.tensor_scalar(score[:, c % 2], score[:, c % 2], L.ext[:, b.slot, c, 0:1], None,
                                                    ALU.add).then_inc(s.shifted.sem, 1)
                            dve.wait_ge(*s.shifted.at(b, c + 1))
                            nc.vector.scalar_tensor_tensor(out=lrelu[:, c % 2], in0=score[:, c % 2], scalar=SLOPE,
                                                           in1=score[:, c % 2], op0=ALU.mult, op1=ALU.max).then_inc(
                                s.lrelu.sem, 1)
                            dve.wait_ge(*s.lrelu.at(b, c + 1))
                            nc.vector.tensor_reduce(minus_max[:, c % 2], lrelu[:, c % 2], AX.X, ALU.max,
                                                    negate=True).then_inc(s.minus_max.sem, 1)

                    def minus_u(b, L):
                        s = sig[L]
                        if factored(L):
                            dve.wait_ge(*s.uvb.at(b, 1))
                            if b.first > 0:
                                dve.wait_ge(*s.above_u.two_back(b))
                            nc.vector.tensor_scalar(L.minus_u[:, b.slot], L.uvb[:, b.slot, 0:C], -1.0, None,
                                                    ALU.mult).then_inc(s.minus_u.sem, 1)

                    def prob_step(b, L, part):
                        if factored(L):
                            prob(b, L, part)
                        elif part == 0:
                            general_prob(b, L)

                    def attend1(b, part):
                        s, L = s1, gat1
                        for c in (2 * part, 2 * part + 1):
                            dve.wait_ge(*s.g_filled.at(b, c + 1))
                            nc.vector.reciprocal(L.recip[:, b.slot, c:c + 1],
                                                 bank[2 + c % 2][:, H:H + 1]).then_inc(s.recip.sem, 1)

                    def negatives1(b, part):
                        s, L = s1, gat1
                        r = slice(2 * part, 2 * part + 2)
                        dve.wait_ge(*s.g_ready.at(b, 2 * part + 2))
                        nc.vector.tensor_scalar(L.neg[:, r], L.y[:, r], 0.0, None, ALU.min).then_inc(s.neg.sem, 1)

                    def elu(b, L, part, parts, used):
                        s = sig[L]
                        r = slice(part * C // parts, (part + 1) * C // parts)
                        dve.wait_ge(*(s.exp if L is gat3 else s.exp2).at(b, part + 1))
                        dve.wait_ge(*used.before(b))
                        nc.vector.scalar_tensor_tensor(out=L.u[:, r], in0=L.neg[:, r], scalar=-1.0, in1=L.y[:, r],
                                                       op0=ALU.add, op1=ALU.max).then_inc(s.u.sem, 1)

                    def residual1(b):
                        for f in range(HT):
                            dve.wait_ge(*z_filled.at(b, f + 1))
                            if b.first > 0 and f == 0:
                                dve.wait_ge(*o2_filled.two_back(b))
                            nc.vector.tensor_tensor(z_t[:, b.slot, f], bank[2 + f][:], o1_t[:, b.slot, f],
                                                    ALU.add).then_inc(z_ready.sem, 1)

                    def attend_masked(b, L, banks, parts):
                        s = sig[L]
                        for q in parts:
                            dve.wait_ge(*s.g_filled.at(b, q + 1))
                            ps = banks[q][:, 0:2 * (D + 2)].rearrange("p (t n) -> p t n", t=2)
                            nc.vector.reciprocal(L.recip[:, b.slot, 2 * q:2 * q + 2], ps[:, :, D]).then_inc(
                                s.recip.sem, 1)

                    def negatives(b, L):
                        s = sig[L]
                        dve.wait_ge(*s.g_ready.at(b, C))
                        nc.vector.tensor_scalar(L.neg[:], L.y[:], 0.0, None, ALU.min).then_inc(s.neg.sem, 1)

                    def norm2(b):
                        dve.wait_ge(*s2.u.at(b, 1))
                        dve.wait_ge(*o2n_filled.at(b, 1))
                        v = gat2.u[:].rearrange("p c n -> p (c n)")
                        nc.vector.tensor_tensor(v, bank[4][:], v, ALU.add).then_inc(v_ready.sem, 1)
                        dve.wait_ge(*v_ready.at(b, 1))
                        dve.wait_ge(*xres_loaded.landed(b))
                        if b.first > 0:
                            dve.wait_ge(*y_ready.two_back(b))
                            dve.wait_ge(*normed_ready[1].two_back(b))
                        nc.vector.scalar_tensor_tensor(out=x1[:, b.slot], in0=gat2.u[:], scalar=0.0,
                                                       in1=x_res[:, b.slot], op0=ALU.max, op1=ALU.add).then_inc(
                            x1_ready.sem, 1)
                        dve.wait_ge(*x1_ready.at(b, 1))
                        moments(b, 1, x1[:, b.slot])

                    steps = {
                        "norm1a": norm1,
                        "norm1b": lambda b: mean_shift(b, 0),
                        "max1": lambda b: maximum(b, gat1),
                        "args1": lambda b: scores(b, gat1),
                        "prob1": lambda b: (prob(b, gat1, 0), prob(b, gat1, 1)),
                        "attend1a": lambda b: attend1(b, 0),
                        "attend1b": lambda b: attend1(b, 1),
                        "exp1a": lambda b: negatives1(b, 0),
                        "exp1b": lambda b: negatives1(b, 1),
                        "elu1a": lambda b: elu(b, gat1, 0, 2, z_filled),
                        "elu1b": lambda b: elu(b, gat1, 1, 2, z_filled),
                        "z": residual1,
                        "max2": lambda b: maximum(b, gat2),
                        "args2": lambda b: scores(b, gat2),
                        "above2": lambda b: minus_u(b, gat2),
                        "prob2a": lambda b: prob_step(b, gat2, 0),
                        "prob2b": lambda b: prob_step(b, gat2, 1),
                        "attend2a": lambda b: attend_masked(b, gat2, (bank[4], bank[5]), (0,)),
                        "attend2b": lambda b: attend_masked(b, gat2, (bank[4], bank[5]), (1,)),
                        "exp2": lambda b: negatives(b, gat2),
                        "elu2": lambda b: elu(b, gat2, 0, 1, x1_ready),
                        "norm2a": norm2,
                        "norm2b": lambda b: mean_shift(b, 1),
                        "max3": lambda b: maximum(b, gat3),
                        "args3": lambda b: scores(b, gat3),
                        "above3": lambda b: minus_u(b, gat3),
                        "prob3a": lambda b: prob_step(b, gat3, 0),
                        "prob3b": lambda b: prob_step(b, gat3, 1),
                        "attend3a": lambda b: attend_masked(b, gat3, (bank[7], bank[6]), (0,)),
                        "attend3b": lambda b: attend_masked(b, gat3, (bank[7], bank[6]), (1,)),
                        "exp3": lambda b: negatives(b, gat3),
                        "elu3": lambda b: elu(b, gat3, 0, 1, y_ready),
                    }
                    with where_needed(dve):
                        run(dve, steps, LAGGED["vector"], {0: guard_ready, 1: lambda dve: (score_weights(dve), masks(dve)), 2: turned_masks})

                @block.tensor
                def _(pe):
                    def mlp1_turn(b):
                        pe.wait_ge(*normed_ready[0].at(b, C))
                        pe.wait_ge(*s1.h_ready.before(b))
                        for c in range(C):
                            last = nc.tensor.transpose(bank[0][:, c * P:(c + 1) * P], normed[0][:, b.slot, c],
                                                       ident[:])
                        last.then_inc(norm_filled[0].sem, 1)

                    def mlp1(b):
                        pe.wait_ge(*norm_t_ready[0].at(b, 1))
                        for f in range(HT):
                            nc.tensor.matmul(bank[1 - f][:], w1_sb[:, f * P:(f + 1) * P], normed_t[0][:, b.slot],
                                             start=True, stop=True).then_inc(o1_filled.sem, 1)

                    def h1(b, part):
                        pe.wait_ge(*o1_ready.at(b, HT))
                        for c in (2 * part, 2 * part + 1):
                            if c >= 2:
                                pe.wait_ge(*s1.h_ready.at(b, c - 1))
                            for k in range(HT):
                                last = nc.tensor.matmul(bank[(c + 1) % 2][:, 0:H + 2],
                                                        o1_t[:, b.slot, k, c * P:(c + 1) * P], wfc_sb[:, k],
                                                        start=(k == 0), stop=(k == HT - 1))
                            last.then_inc(s1.h_filled.sem, 1)

                    def attend1(b, part):
                        for c in (2 * part, 2 * part + 1):
                            if c == 0:
                                pe.wait_ge(*o2_ready.before(b))
                                pe.wait_ge(*s1.h_ready.at(b, C))
                            elif c == 1:
                                pe.wait_ge(*z_ready.before(b))
                            else:
                                pe.wait_ge(*s1.g_ready.at(b, c - 1))
                            for t in range(C):
                                if c == 0:
                                    pe.wait_ge(*s1.prob_ready.at(b, t + 1))
                                last = nc.tensor.matmul(bank[2 + c % 2][:, 0:H + 1],
                                                        gat1.prob[:, b.slot, t, c * P:(c + 1) * P],
                                                        gat1.ext[:, b.slot, t, 2:H + 3],
                                                        start=(t == 0), stop=(t == C - 1))
                            last.then_inc(s1.g_filled.sem, 1)

                    def z(b):
                        pe.wait_ge(*s1.u.at(b, 2))
                        for f in range(HT):
                            pe.wait_ge(*s1.g_ready.at(b, 3 + f))
                            for c in range(C):
                                last = nc.tensor.transpose(bank[2 + f][:, c * P:(c + 1) * P],
                                                           gat1.u[:, c, f * P:(f + 1) * P], ident[:])
                            last.then_inc(z_filled.sem, 1)

                    def mlp2(b):
                        pe.wait_ge(*z_ready.at(b, HT))
                        for k in range(HT):
                            last = nc.tensor.matmul(bank[2][:], w2_sb[:, k], z_t[:, b.slot, k],
                                                    start=(k == 0), stop=(k == HT - 1))
                        last.then_inc(o2_filled.sem, 1)

                    def h_masked(b, L, src, banks):
                        s = sig[L]
                        for q in range(C // 2):
                            for e in range(2):
                                c = 2 * q + e
                                last = nc.tensor.matmul(banks[q][:, e * (D + 2):(e + 1) * (D + 2)],
                                                        src[:, c * P:(c + 1) * P], L.w[:, 0], start=True, stop=True)
                            last.then_inc(s.h_filled.sem, 1)

                    def h2(b):
                        pe.wait_ge(*o2_ready.at(b, 1))
                        pe.wait_ge(*v_ready.before(b))
                        pe.wait_ge(*s2.g_ready.before(b))
                        h_masked(b, gat2, o2_t[:, b.slot], (bank[4], bank[5]))

                    def turn2(b):
                        pe.wait_ge(*normed_ready[1].at(b, C))
                        pe.wait_ge(*s3.g_ready.before(b))
                        for c in range(C):
                            last = nc.tensor.transpose(bank[6][:, c * P:(c + 1) * P], normed[1][:, b.slot, c],
                                                       ident[:])
                        last.then_inc(norm_filled[1].sem, 1)

                    def h3(b):
                        pe.wait_ge(*norm_t_ready[1].at(b, 1))
                        h_masked(b, gat3, normed_t[1][:, b.slot], (bank[7], bank[6]))

                    def general_prob(b, L, banks):
                        s = sig[L]
                        for c in range(C):
                            pe.wait_ge(*s.prob_n.at(b, c + 1))
                            if c < 2:
                                pe.wait_ge(*s.h_ready.at(b, c + 1))
                            else:
                                pe.wait_ge(*s.prob_ready.at(b, c - 1))
                            for t in range(C):
                                last = nc.tensor.transpose(banks[c % 2][:, t * P:(t + 1) * P],
                                                           prob_n[:, c % 2, t:N:C], ident[:])
                            last.then_inc(s.prob_filled.sem, 1)

                    def attend_masked(b, L, banks, parts):
                        s = sig[L]
                        if 0 in parts:
                            pe.wait_ge(*s.h_ready.at(b, 2))
                            if not factored(L):
                                pe.wait_ge(*s.prob_ready.at(b, C))
                        for q in parts:
                            for e in range(2):
                                c = 2 * q + e
                                for t in range(C):
                                    if c == 0 and factored(L):
                                        pe.wait_ge(*s.prob_ready.at(b, t + 1))
                                    last = nc.tensor.matmul(banks[q][:, e * (D + 2):e * (D + 2) + D + 1],
                                                            L.prob[:, b.slot, t, c * P:(c + 1) * P],
                                                            L.ext[:, b.slot, t, 2:D + 3],
                                                            start=(t == 0), stop=(t == C - 1))
                            last.then_inc(s.g_filled.sem, 1)

                    def turn_o2(b):
                        pe.wait_ge(*s2.g_ready.at(b, 2))
                        for c in range(C):
                            last = nc.tensor.transpose(bank[4][:, c * P:(c + 1) * P],
                                                       o2_t[:, b.slot, c * P:(c + 1) * P], ident[:])
                        last.then_inc(o2n_filled.sem, 1)

                    steps = {
                        "mlp1_turn": mlp1_turn,
                        "mlp1": mlp1,
                        "h1a": lambda b: h1(b, 0),
                        "h1b": lambda b: h1(b, 1),
                        "attend1a": lambda b: attend1(b, 0),
                        "attend1b": lambda b: attend1(b, 1),
                        "z": z,
                        "mlp2": mlp2,
                        "h2": h2,
                        "prob2a": (lambda b: general_prob(b, gat2, (bank[4], bank[5]))) if general else (lambda b: None),
                        "attend2a": lambda b: attend_masked(b, gat2, (bank[4], bank[5]), (0,)),
                        "attend2b": lambda b: attend_masked(b, gat2, (bank[4], bank[5]), (1,)),
                        "turn_o2": turn_o2,
                        "turn2": turn2,
                        "h3": h3,
                        "prob3a": (lambda b: general_prob(b, gat3, (bank[7], bank[6]))) if general else (lambda b: None),
                        "attend3a": lambda b: attend_masked(b, gat3, (bank[7], bank[6]), (0,)),
                        "attend3b": lambda b: attend_masked(b, gat3, (bank[7], bank[6]), (1,)),
                    }
                    with where_needed(pe):
                        run(pe, steps, LAGGED["tensor"], {0: weights_ready, 1: score_weights_ready, 2: turn_masks})

        network(general=False, pipelined=True, passed=0)

        s_guard = semaphore("guard_reduced")
        s_spread = semaphore("guard_over_partitions")
        s_flag = semaphore("guard_flag")

        with nc.Block() as block:
            @block.vector
            def _(dve):
                nc.vector.tensor_reduce(guard_col[:], guard[:], AX.XY, ALU.min, negate=True).then_inc(s_guard, 1)
                dve.wait_ge(s_spread, 1)
                nc.vector.tensor_scalar(guard_flag[:], guard_all[:], RANGE_LIMIT, None, ALU.is_gt).then_inc(s_flag, 1)
                dve.wait_ge(s_flag, 1)

            @block.gpsimd
            def _(pool):
                pool.wait_ge(s_guard, 1)
                nc.gpsimd.partition_all_reduce(guard_all[:], guard_col[:], P,
                                               bass.bass_isa.ReduceOp.max).then_inc(s_spread, 1)

        network(general=True, pipelined=False, passed=B)


_INS = ['x', 'adj', 'L0_gnn_mlp1_w', 'L0_gnn_mlp1_b', 'L0_gnn_mlp2_w', 'L0_gnn_mlp2_b', 'L0_gnn_W_fc', 'L0_gnn_a_fc',
        'L0_gnn_W_hand', 'L0_gnn_a_hand', 'L1_gnn_W', 'L1_gnn_a']
_OUTS = [((16, 512, 128), 'float32')]


def kernel(**inputs):
    import numpy as _np
    import concourse.bacc as _bacc
    from concourse import mybir as _mybir
    from concourse.bass_utils import run_bass_kernel_spmd as _run

    nc = _bacc.Bacc("TRN2", target_bir_lowering=False, num_devices=1)
    arrays, args = {}, []
    for name in _INS:
        a = _np.ascontiguousarray(inputs[name])
        arrays[f"in_{name}"] = a
        args.append(nc.dram_tensor(f"in_{name}", a.shape, _mybir.dt.from_np(a.dtype), kind="ExternalInput").ap())
    for i, (shape, dtype) in enumerate(_OUTS):
        dt = _mybir.dt.from_np(_np.dtype(dtype))
        args.append(nc.dram_tensor(f"out_{i}", shape, dt, kind="ExternalOutput").ap())
    gnn_program(nc, *args)
    r = _run(nc, [arrays], core_ids=[0])
    return r.results[0]["out_0"]
```
